# Optimizing a Trainium2 kernel written in Bass

```python
import numpy as np
import jax
import jax.numpy as jnp

def _softmax(x, axis=-1):
    return jax.nn.softmax(x, axis=axis)

def _gelu(x):
    return jax.nn.gelu(x, approximate=True)

def _silu(x):
    return jax.nn.silu(x)

def _sigmoid(x):
    return jax.nn.sigmoid(x)

def _layernorm(x, axis=-1, eps=1e-05):
    m = jnp.mean(x, axis=axis, keepdims=True)
    v = jnp.var(x, axis=axis, keepdims=True)
    return (x - m) / jnp.sqrt(v + eps)

def _scatter_add(tgt, idx, src, axis=0):
    return tgt.at[idx].add(src)

def _segment_sum(src, seg, n):
    return jax.ops.segment_sum(src, seg, n)
kernel_name = 'mk_gnn_ffn_d1_gnn_r8_7fe556'

def setup_inputs(seed: int=0):
    np.random.seed(seed)
    _w = jnp.asarray

    def _rec_inputs():
        import jax
        import jax.numpy as jnp
        _gk = jax.random.key(seed)
        x = -0.0002117 + 1 * jax.random.normal(jax.random.fold_in(_gk, 1), (6250, 512), jnp.float32)
        _s = jax.random.randint(jax.random.fold_in(_gk, 2), (50000,), 0, 6250, jnp.int32)
        _d = jax.random.randint(jax.random.fold_in(_gk, 3), (50000,), 0, 6250, jnp.int32)
        _loop = jnp.arange(6250, dtype=jnp.int32)
        src = jnp.concatenate([_s, _d, _loop])
        dst = jnp.concatenate([_d, _s, _loop])
        _o = jnp.argsort(dst, stable=True)
        src = src[_o]
        dst = dst[_o]
        return (x, src, dst)
    x, src, dst = _rec_inputs()

    def _L0_gnn_setup():
        import jax, jax.numpy as jnp
        import numpy as np
        N = 6250
        E = 50000
        D_IN = 512
        D_OUT = 512
        LN_EPS = 1e-05
        key = jax.random.key(seed)
        ks = jax.random.split(key, 8)
        x = jax.random.normal(ks[0], (N, D_IN), dtype=jnp.float32)
        src = jax.random.randint(ks[1], (E,), 0, N, dtype=jnp.int32)
        dst = jnp.sort(jax.random.randint(ks[2], (E,), 0, N, dtype=jnp.int32))
        bound = 1.0 / np.sqrt(D_IN)
        W_self = jax.random.uniform(ks[3], (D_IN, D_OUT), minval=-bound, maxval=bound, dtype=jnp.float32)
        b_self = jax.random.uniform(ks[4], (D_OUT,), minval=-bound, maxval=bound, dtype=jnp.float32)
        W_neigh = jax.random.uniform(ks[5], (D_IN, D_OUT), minval=-bound, maxval=bound, dtype=jnp.float32)
        gamma = jnp.ones((D_OUT,), dtype=jnp.float32)
        beta = jnp.zeros((D_OUT,), dtype=jnp.float32)
        alpha = jnp.array(0.25, dtype=jnp.float32)
        return {'x': x, 'src': src, 'dst': dst, 'W_self': W_self, 'b_self': b_self, 'W_neigh': W_neigh, 'gamma': gamma, 'beta': beta, 'alpha': alpha}
    _L0_gnn_all = _L0_gnn_setup()
    _L0_gnn_in = {k: v for k, v in _L0_gnn_all.items() if k in ('W_self', 'b_self', 'W_neigh', 'gamma', 'beta', 'alpha')}
    del _L0_gnn_all

    def _L0_ffn_setup():
        import jax, jax.numpy as jnp
        import numpy as np
        DIM = 512
        FFN_DIM = 1408
        GROUP = 128
        EPS = 1e-05

        def _quantize_weight(w, group_size):
            o, i = w.shape
            wg = w.reshape(o, i // group_size, group_size)
            scale = jnp.mean(jnp.abs(wg), axis=-1, keepdims=True) + EPS
            wq = jnp.clip(jnp.round(wg / scale), -1.0, 1.0) * scale
            return wq.reshape(o, i)

        def _bitlinear(x, w, group_size=GROUP):
            wq = w + jax.lax.stop_gradient(_quantize_weight(w, group_size) - w)
            return jnp.einsum('bsd,fd->bsf', x, wq)
        key = jax.random.key(seed)
        k_x, k_g, k_u, k_d = jax.random.split(key, 4)
        x = jax.random.normal(k_x, (8, 512, DIM), dtype=jnp.float32)
        sd_in = 1.0 / np.sqrt(DIM)
        sd_ffn = 1.0 / np.sqrt(FFN_DIM)
        w_gate = jax.random.normal(k_g, (FFN_DIM, DIM), dtype=jnp.float32) * sd_in
        w_up = jax.random.normal(k_u, (FFN_DIM, DIM), dtype=jnp.float32) * sd_in
        w_down = jax.random.normal(k_d, (DIM, FFN_DIM), dtype=jnp.float32) * sd_ffn
        return {'x': x, 'w_gate': w_gate, 'w_up': w_up, 'w_down': w_down}
    _L0_ffn_all = _L0_ffn_setup()
    _L0_ffn_in = {k: v for k, v in _L0_ffn_all.items() if k in ('w_gate', 'w_up', 'w_down')}
    del _L0_ffn_all
    return {'x': x, 'src': src, 'dst': dst, 'L0_gnn_W_self': _L0_gnn_in['W_self'], 'L0_gnn_b_self': _L0_gnn_in['b_self'], 'L0_gnn_W_neigh': _L0_gnn_in['W_neigh'], 'L0_gnn_gamma': _L0_gnn_in['gamma'], 'L0_gnn_beta': _L0_gnn_in['beta'], 'L0_gnn_alpha': _L0_gnn_in['alpha'], 'L0_ffn_w_gate': _L0_ffn_in['w_gate'], 'L0_ffn_w_up': _L0_ffn_in['w_up'], 'L0_ffn_w_down': _L0_ffn_in['w_down']}

def reference(x, src, dst, L0_gnn_W_self, L0_gnn_b_self, L0_gnn_W_neigh, L0_gnn_gamma, L0_gnn_beta, L0_gnn_alpha, L0_ffn_w_gate, L0_ffn_w_up, L0_ffn_w_down):
    import jax
    import jax.numpy as jnp

    def _L0_gnn_ref(x, src, dst, W_self, b_self, W_neigh, gamma, beta, alpha):
        import jax, jax.numpy as jnp
        import numpy as np
        N = 6250
        E = 50000
        D_IN = 512
        D_OUT = 512
        LN_EPS = 1e-05
        deg = jax.ops.segment_sum(jnp.ones_like(src, dtype=x.dtype), dst, num_segments=N)
        inv_deg = 1.0 / jnp.maximum(deg, 1.0)
        agg = jax.ops.segment_sum(x[src], dst, num_segments=N)
        neigh = agg * inv_deg[:, None]
        h = x @ W_self + b_self + neigh @ W_neigh
        mu = jnp.mean(h, axis=-1, keepdims=True)
        var = jnp.mean(jnp.square(h - mu), axis=-1, keepdims=True)
        h = (h - mu) * jax.lax.rsqrt(var + LN_EPS) * gamma + beta
        h = jnp.where(h >= 0, h, alpha * h)
        return h + x

    def _L0_ffn_ref(x, w_gate, w_up, w_down):
        import jax, jax.numpy as jnp
        import numpy as np
        DIM = 512
        FFN_DIM = 1408
        GROUP = 128
        EPS = 1e-05

        def _quantize_weight(w, group_size):
            o, i = w.shape
            wg = w.reshape(o, i // group_size, group_size)
            scale = jnp.mean(jnp.abs(wg), axis=-1, keepdims=True) + EPS
            wq = jnp.clip(jnp.round(wg / scale), -1.0, 1.0) * scale
            return wq.reshape(o, i)

        def _bitlinear(x, w, group_size=GROUP):
            wq = w + jax.lax.stop_gradient(_quantize_weight(w, group_size) - w)
            return jnp.einsum('bsd,fd->bsf', x, wq)
        gate = _bitlinear(x, w_gate)
        up = _bitlinear(x, w_up)
        h = jax.nn.silu(gate) * up
        return _bitlinear(h, w_down)
    x = x + _L0_gnn_ref(_layernorm(x, axis=-1), src, dst, L0_gnn_W_self, L0_gnn_b_self, L0_gnn_W_neigh, L0_gnn_gamma, L0_gnn_beta, L0_gnn_alpha)
    x = x + _L0_ffn_ref(_layernorm(x, axis=-1)[None], L0_ffn_w_gate, L0_ffn_w_up, L0_ffn_w_down)[0]
    return x

_drawn_inputs = setup_inputs


def setup_inputs(seed=0):
    import zlib

    import numpy as np

    out = dict(_drawn_inputs(seed))
    spreads = {'L0_gnn_gamma': (1.0, 0.2), 'L0_gnn_beta': (0.0, 0.1)}
    factors = {'L0_gnn_b_self': 3.908}
    for name, (base, spread) in spreads.items():
        noise = np.random.default_rng([zlib.crc32(name.encode()), seed]).standard_normal(out[name].shape)
        drawn = base * np.exp(spread * noise) if base else spread * noise
        out[name] = jnp.asarray(drawn.astype(out[name].dtype))
    for name, factor in factors.items():
        out[name] = (out[name] * factor).astype(out[name].dtype)
    return out
```

```python
from contextlib import ExitStack

import numpy as np

import concourse.bass as bass
from concourse import mybir

ALU = mybir.AluOpType
ACT = mybir.ActivationFunctionType
F32 = mybir.dt.float32
F16 = mybir.dt.float16
BF16 = mybir.dt.bfloat16
I32 = mybir.dt.int32
AX = mybir.AxisListType
RMAX = bass.bass_isa.ReduceOp.max

P = 128
EPS = 1e-5
XSCALE = 1024.0
RSQRT_GUESS = float(0x5F3759DF - (1 << 31))
EXPONENT_BITS = 0x7F800000
TWICE_BIAS_BITS = float(0x7F000000)
STEPS = 18
PER_LOAD = 3
LOADS = STEPS // PER_LOAD
BIG = float(1 << 17)


def build(nc, x, src, dst, W_self, b_self, W_neigh, gamma, beta, alpha, w_gate, w_up, w_down, out):
    N, D = x.shape
    E = src.shape[0]
    FFN = w_gate.shape[0]
    KT = D // P
    FT = FFN // P
    NG = FT * KT
    BLOCKS = -(-N // P)
    LAST = N - (BLOCKS - 1) * P
    CHUNK = 4
    CW = CHUNK * P
    FULL = (BLOCKS - 1) // CHUNK
    assert BLOCKS == FULL * CHUNK + 1 and FULL % 2 == 0 and D == CW
    PASS = STEPS * P
    EP = 125
    SEG = 17
    EROW = E // EP
    NSEG = EROW // SEG
    assert EP * NSEG * SEG == E
    GROUP = 7
    GROUPS = BLOCKS // GROUP
    assert GROUP * GROUPS == BLOCKS

    table = nc.dram_tensor("node_table", (N, 2 * D), F16, kind="Internal").ap()
    src_pad = nc.dram_tensor("src_pad", (E + PASS,), I32, kind="Internal").ap()
    dst_pad = nc.dram_tensor("dst_pad", (E + PASS,), F32, kind="Internal").ap()

    with ExitStack() as ctx:
        def sb(name, shape, dt):
            return ctx.enter_context(nc.sbuf_tensor(name, shape, dt))

        def bank(name):
            return ctx.enter_context(nc.psum_tensor(name, [P, 512], F32))

        sems = {}

        def sem(name):
            sems[name] = ctx.enter_context(nc.semaphore(name))
            return sems[name]

        rows = sb("rows", [P, STEPS, 2 * D], F16)
        wself = sb("wself", [P, KT, D], F32)
        wneigh = sb("wneigh", [P, KT, D], F32)
        tern = sb("tern", [P, 3, NG, P], F16)
        x1 = sb("x1", [P, 2, CHUNK, D], F32)
        x1T = sb("x1T", [P, 2, 2, KT, CW], F16)
        hT = sb("hT", [P, 2, FT, CW], F16)
        yT = sb("yT", [P, KT, CW], F32)
        acc = sb("acc", [P, 2, 2, CW], F32)
        xin = sb("xin", [P, 2, D], F32)
        xs = sb("xs", [P, D], F32)
        xx = sb("xx", [P, D], F32)
        t2 = sb("t2", [P, D], F32)
        x1s = sb("x1s", [P, D], F32)
        outb = sb("outb", [P, 2, D], F32)
        xsT = sb("xsT", [P, KT, P], F32)
        ng = sb("ng", [P, D], F32)
        ngT = sb("ngT", [P, KT, P], F32)
        gamma_b = sb("gamma_b", [P, D], F32)
        beta_b = sb("beta_b", [P, D], F32)
        hot = sb("hot", [P, P, STEPS], F16)
        node_j = sb("node_j", [P, P, STEPS], F16)
        idx = sb("idx", [P, STEPS], I32)
        dstv = sb("dstv", [P, STEPS], F32)
        dstl = sb("dstl", [P, STEPS], F16)
        identf = sb("identf", [P, P], F32)
        ident = sb("ident", [P, 2, P], F16)
        zeros = sb("zeros", [P, P], F16)
        ones = sb("ones", [P, P], F16)
        bparts = sb("bparts", [3, D], BF16)
        onesb = sb("onesb", [3, P], BF16)
        alpha_c = sb("alpha_c", [P, 1], F32)
        neg_alpha = sb("neg_alpha", [P, 1], F32)
        base = sb("base", [P, BLOCKS], F32)
        top = sb("top", [P, BLOCKS], F32)
        stats6 = sb("stats6", [P, GROUP, 6], F32)
        mv = sb("mv", [P, BLOCKS, 2], F32)
        rstd = sb("rstd", [P, BLOCKS], F32)
        nmr = sb("nmr", [P, BLOCKS], F32)
        rstd_k = sb("rstd_k", [P, BLOCKS], F32)
        nmr_k = sb("nmr_k", [P, BLOCKS], F32)
        one_r = sb("one_r", [P, BLOCKS], F32)
        tmp = sb("tmp", [P, 4, GROUP], F32)
        small = sb("small", [P, 32], F32)
        st6 = sb("st6", [P, 6], F32)
        segs = sb("segs", [P, 4, NSEG], F32)
        posi = sb("posi", [P, NSEG], I32)
        ranges = sb("ranges", [P, 2 * BLOCKS], F32)
        rangem = sb("rangem", [P, 2 * BLOCKS], F32)
        rangei = sb("rangei", [P, 2 * BLOCKS], I32)
        padi = sb("padi", [P, STEPS], I32)
        padf = sb("padf", [P, STEPS], F32)
        scl = sb("scl", [P, 3, NG], F32)
        half = sb("half", [P, 2, NG], F32)
        wmax = sb("wmax", [P, 2], F32)
        wmaxa = sb("wmaxa", [P, 2], F32)
        hsc = sb("hsc", [P, 4], F32)

        agg_ps = bank("agg_ps")
        h_ps = bank("h_ps")
        tr_ps = bank("tr_ps")
        misc_ps = bank("misc_ps")
        f_ps = [bank(f"f_ps{i}") for i in range(4)]

        xgroup = rows[:, :, :].rearrange("p a b -> p (a b)").bitcast(F32)[:, 0:2 * GROUP * D].rearrange(
            "p (g t d) -> p g t d", g=2, t=GROUP)
        tstage = [x1[:, :, :, :].rearrange("p a b c -> p (a b c)").bitcast(F16)[:, 0:GROUP * 2 * D].rearrange(
            "p (t d) -> p t d", t=GROUP),
            x1T[:, :, :, :, :].rearrange("p a b c d -> p (a b c d)")[:, 0:GROUP * 2 * D].rearrange(
            "p (t d) -> p t d", t=GROUP)]
        wstage = hT[:, :, :, :].rearrange("p a b c -> p (a b c)").bitcast(F32).rearrange(
            "p (g k) -> p g k", g=NG)
        above = x1[:, :, :, :].rearrange("p a b c -> p (a b c)").bitcast(F16)[:, 0:NG * P].rearrange(
            "p (g k) -> p g k", g=NG)
        below = x1T[:, :, :, :, :].rearrange("p a b c d -> p (a b c d)")[:, 0:NG * P].rearrange(
            "p (g k) -> p g k", g=NG)
        tern32 = tern[:, :, :, :].rearrange("p w g k -> p w (g k)").bitcast(F32)
        hit = [tern32[0:EP, w, 0:BLOCKS * NSEG].rearrange("p (b s) -> p b s", b=BLOCKS) for w in range(3)]
        yflat = yT[:, :, :].rearrange("p a b -> p (a b)")
        dst_i = yflat[0:EP, 0:EROW].bitcast(I32)
        dst_f = yflat[0:EP, EROW:2 * EROW]

        brow = acc[0:1, :, :, :].rearrange("p a b c -> p (a b) c")
        browb = outb[0:1, :, :].rearrange("p a b -> p (a b)").bitcast(BF16)[:, 0:3 * D].rearrange("p (i d) -> p i d", i=3)

        ld_dst, ld_const, ld_bias, ld_pads = sem("ld_dst"), sem("ld_const"), sem("ld_bias"), sem("ld_pads")
        ld_w = [sem(f"ld_w{w}") for w in range(3)]
        ld_xg = [sem(f"ld_xg{i}") for i in range(2)]
        st_t = [sem(f"st_t{i}") for i in range(2)]
        ld_x = [sem(f"ld_x{i}") for i in range(2)]
        ld_idx, ld_dv = sem("ld_idx"), sem("ld_dv")
        gathered = [sem(f"gathered{i}") for i in range(LOADS)]
        st_out = sem("st_out")
        pool_c, pool_rng, pool_max = sem("pool_c"), sem("pool_rng"), sem("pool_max")
        v_pro, v_dst, v_rng, v_rngi, v_bias = sem("v_pro"), sem("v_dst"), sem("v_rng"), sem("v_rngi"), sem("v_bias")
        v_stat, v_low, v_cmp, v_max, v_scl = sem("v_stat"), sem("v_low"), sem("v_cmp"), sem("v_max"), sem("v_scl")
        a_norm, a_high, p_tern, a_tern = sem("a_norm"), sem("a_high"), sem("p_tern"), sem("a_tern")
        v_xs, v_xx, v_dl, v_hot, v_inv, v_chain = (sem(n) for n in ("v_xs", "v_xx", "v_dl", "v_hot", "v_inv", "v_chain"))
        v_t2, v_x1, v_x1s, v_lo1 = (sem(n) for n in ("v_t2", "v_x1", "v_x1s", "v_lo1"))
        p_t1, p_used, p_agg, p_t2, p_h, p_t3 = (sem(n) for n in ("p_t1", "p_used", "p_agg", "p_t2", "p_h", "p_t3"))
        a_xsT, a_ng, a_ngT, a_y, a_hi1 = (sem(n) for n in ("a_xsT", "a_ng", "a_ngT", "a_y", "a_hi1"))
        p_gu, p_dn, p_t4 = (sem(n) for n in ("p_gu", "p_dn", "p_t4"))
        a_gu, a_silu, a_hi, a_dn = (sem(n) for n in ("a_gu", "a_silu", "a_hi", "a_dn"))
        v_gu, v_h, v_lo, v_dn, v_out = (sem(n) for n in ("v_gu", "v_h", "v_lo", "v_dn", "v_out"))
        stored = sem("stored")
        sp_turn, pool_turn, dve_turn = sem("sp_turn"), sem("pool_turn"), sem("dve_turn")

        def done(eng, s, n):
            eng.wait_ge(s, n + 1)

        def first_credit(eng, names):
            for name in names:
                eng.sem_inc(sems[name], 1)

        def walk(block, ffn, tail):
            for q in range(CHUNK):
                block(0, q, 0, None)
            yield_loop = (FULL - 2) // 2
            return yield_loop

        def main(eng, block):
            for q in range(CHUNK):
                block(0, q, 0, [])
            with eng.Fori(0, (FULL - 2) // 2) as u:
                for h in range(2):
                    for q in range(CHUNK):
                        block(u * 2 + (1 + h), q, (1 + h) % 2, [q])
            for q in range(CHUNK):
                block(FULL - 1, q, (FULL - 1) % 2, [q])
            block(FULL, 0, FULL % 2, [0, 1, 2, 3])

        QF = [range(0, 4), range(4, 8), range(8, FT), range(0, 0)]
        QD = [range(0, 0), range(0, 0), range(0, 1), range(1, KT)]
        F_AFTER = [4, 8, FT, FT]

        block_ctx = ctx.enter_context(nc.Block())

        @block_ctx.sync
        def _(sp):
            first_credit(sp, ["stored"])
            sp.dma_start(dst_i, dst.rearrange("(p e) -> p e", p=EP)).then_inc(ld_dst, 16)

            def load_group(g):
                if g >= 2:
                    done(sp, a_norm, GROUP * (g - 1))
                    sp.wait_ge(v_stat, g - 1)
                if g < GROUPS - 1:
                    sp.dma_start(xgroup[:, g % 2], x[g * GROUP * P:(g + 1) * GROUP * P, :].rearrange(
                        "(t p) d -> p t d", p=P)).then_inc(ld_xg[g % 2], 16)
                else:
                    r0 = g * GROUP * P
                    sp.dma_start(xgroup[:, g % 2, 0:GROUP - 1], x[r0:r0 + (GROUP - 1) * P, :].rearrange(
                        "(t p) d -> p t d", p=P)).then_inc(ld_xg[g % 2], 16)
                    sp.dma_start(xgroup[0:LAST, g % 2, GROUP - 1], x[N - LAST:N, :]).then_inc(ld_xg[g % 2], 16)

            load_group(0)
            load_group(1)
            sp.dma_start(src_pad[0:E].rearrange("(p e) -> p e", p=EP), src.rearrange("(p e) -> p e", p=EP)).then_inc(ld_pads, 16)
            sp.wait_ge(pool_c, 1)
            sp.dma_start(src_pad[E:E + PASS].rearrange("(p e) -> p e", p=P), padi[:, :]).then_inc(ld_pads, 16)
            sp.dma_start(dst_pad[E:E + PASS].rearrange("(p e) -> p e", p=P), padf[:, :]).then_inc(ld_pads, 16)
            sp.wait_ge(v_dst, 1)
            sp.dma_start(dst_pad[0:E].rearrange("(p e) -> p e", p=EP), dst_f).then_inc(ld_pads, 16)
            sp.dma_start(brow[:, 0, :], b_self.rearrange("(a d) -> a d", a=1)).then_inc(ld_bias, 16)
            load_group(2)
            sp.dma_start(gamma_b[:, :], gamma.rearrange("(a d) -> a d", a=1).broadcast_to((P, D))).then_inc(ld_const, 16)
            sp.dma_start(beta_b[:, :], beta.rearrange("(a d) -> a d", a=1).broadcast_to((P, D))).then_inc(ld_const, 16)
            sp.dma_start(alpha_c[:, :], alpha.rearrange("(a d) -> a d", a=1).broadcast_to((P, 1))).then_inc(ld_const, 16)
            sp.dma_start(wself[:, :, :], W_self.rearrange("(k p) n -> p k n", p=P)).then_inc(ld_const, 16)
            sp.dma_start(wneigh[:, :, :], W_neigh.rearrange("(k p) n -> p k n", p=P)).then_inc(ld_const, 16)
            sp.wait_ge(v_bias, 1)
            for i in range(3):
                sp.dma_start(bparts[i:i + 1, :], browb[:, i, :]).then_inc(ld_bias, 16)
            sp.dma_start(wstage, w_gate.rearrange("(i p) (g k) -> p i g k", p=P, k=P)).then_inc(ld_w[0], 16)
            for g in range(GROUPS):
                if g + 3 < GROUPS:
                    load_group(g + 3)
                done(sp, v_low, GROUP * (g + 1))
                if g < GROUPS - 1:
                    sp.dma_start(table[g * GROUP * P:(g + 1) * GROUP * P, :].rearrange("(t p) d -> p t d", p=P),
                                 tstage[g % 2]).then_inc(st_t[g % 2], 16)
                else:
                    r0 = g * GROUP * P
                    sp.dma_start(table[r0:r0 + (GROUP - 1) * P, :].rearrange("(t p) d -> p t d", p=P),
                                 tstage[g % 2][:, 0:GROUP - 1]).then_inc(st_t[g % 2], 16)
                    sp.dma_start(table[N - LAST:N, :], tstage[g % 2][0:LAST, GROUP - 1]).then_inc(st_t[g % 2], 16)
            sp.wait_ge(ld_pads, 64)
            sp.wait_ge(v_rngi, 1)
            passes = sp.alloc_register("sp_passes")
            sp.reg_mov(passes, 0)

            def load_edges(b):
                first = sp.value_load(rangei[0:1, bass.ds(b, 1)], min_val=0, max_val=E)
                end = sp.value_load(rangei[0:1, bass.ds(b + BLOCKS, 1)], min_val=0, max_val=E)
                with sp.Fori(first, end, PASS) as at:
                    n = sp.snap(passes)
                    sp.wait_ge(p_used, n * LOADS + LOADS)
                    sp.sem_inc(sp_turn, 1)
                    done(sp, v_dl, n)
                    sp.sem_inc(sp_turn, 1)
                    sp.dma_start(idx[:, :], src_pad[bass.ds(at, PASS)].rearrange("(p e) -> p e", p=P)).then_inc(ld_idx, 16)
                    sp.dma_start(dstv[:, :], dst_pad[bass.ds(at, PASS)].rearrange("(p e) -> p e", p=P)).then_inc(ld_dv, 16)
                    sp.reg_add(passes, passes, 1)

            def load_x(b, q):
                row = b * P if isinstance(b, int) else sp.snap(b * P)
                done(sp, v_xx, b - 1 if not isinstance(b, int) else max(b - 1, 0))
                if isinstance(b, int) and b == BLOCKS - 1:
                    sp.dma_start(xin[0:LAST, q % 2], x[N - LAST:N, :]).then_inc(ld_x[q % 2], 16)
                else:
                    sp.dma_start(xin[:, q % 2], x[bass.ds(row, P), :]).then_inc(ld_x[q % 2], 16)

            load_x(0, 0)
            load_edges(0)

            def store_out(c, q, rows_):
                row = (c * CHUNK + q) * P if isinstance(c, int) else sp.snap((c * CHUNK + q) * P)
                done(sp, v_out, c * CHUNK + q + 1)
                sp.dma_start(out[bass.ds(row, rows_), :], outb[0:rows_, q % 2]).then_inc(st_out, 16)
                sp.wait_ge(st_out, c * (16 * CHUNK) + (16 * q + 16))
                sp.sem_inc(stored, 1)

            def block(c, q, par, ffns):
                b = c * CHUNK + q
                if not (isinstance(b, int) and b == BLOCKS - 1):
                    load_x(b + 1, q + 1)
                    load_edges(b + 1)
                if 3 in ffns:
                    for qq in range(CHUNK):
                        store_out(c - 1, qq, P)

            sp.wait_ge(v_cmp, FT)
            sp.dma_start(wstage, w_up.rearrange("(i p) (g k) -> p i g k", p=P, k=P)).then_inc(ld_w[1], 16)
            sp.wait_ge(v_cmp, 2 * FT)
            sp.dma_start(wstage, w_down.rearrange("(i p) (g k) -> p i g k", p=P, k=P)).then_inc(ld_w[2], 16)
            main(sp, block)
            store_out(FULL, 0, LAST)

        @block_ctx.gpsimd
        def _(pool):
            pool.memset(padi[:, :], 0)
            pool.memset(padf[:, :], -1.0).then_inc(pool_c, 1)
            pool.memset(ones[:, :], 1.0)
            pool.memset(onesb[:, :], 1.0)
            pool.memset(zeros[:, :], 0.0)
            pool.memset(xin[:, :, :], 0.0)
            pool.memset(ranges[:, :], 0.0)
            pool.memset(identf[:, :], 0.0)
            pool.memset(ident[:, :, :], 0.0).then_inc(pool_c, 1)
            pool.iota(padi_scratch := rangei[:, 0:BLOCKS], pattern=[[P, BLOCKS]], base=0, channel_multiplier=0)
            pool.iota(posi[:, :], pattern=[[SEG, NSEG]], base=0, channel_multiplier=EROW)
            pool.iota(node_j[:, :, :], pattern=[[1, P], [0, STEPS]], base=0, channel_multiplier=0,
                      allow_small_or_imprecise_dtypes=True)
            pool.wait_ge(pool_c, 2)
            pool.affine_select(out=identf[:, :], in_=identf[:, :], compare_op=ALU.not_equal, fill=1.0, base=0,
                               pattern=[[-1, P]], channel_multiplier=1)
            pool.affine_select(out=ident[:, 0, :], in_=ident[:, 0, :], compare_op=ALU.not_equal, fill=1.0, base=0,
                               pattern=[[-1, P]], channel_multiplier=1)
            pool.affine_select(out=ident[:, 1, :], in_=ident[:, 1, :], compare_op=ALU.not_equal, fill=-1.0, base=0,
                               pattern=[[-1, P]], channel_multiplier=1).then_inc(pool_c, 1)
            pool.wait_ge(v_rng, 1)
            pool.partition_all_reduce(rangem[:, :], ranges[:, :], P, RMAX).then_inc(pool_rng, 1)
            pool.wait_ge(v_rngi, 1)
            pool.wait_ge(st_t[0], 16 * ((GROUPS + 1) // 2) + 16 * (GROUPS % 2))
            pool.wait_ge(st_t[1], 16 * (GROUPS // 2) + 16 * ((GROUPS + 1) % 2))
            passes = pool.alloc_register("pool_passes")
            pool.reg_mov(passes, 0)

            def gather(b):
                first = pool.value_load(rangei[0:1, bass.ds(b, 1)], min_val=0, max_val=E)
                end = pool.value_load(rangei[0:1, bass.ds(b + BLOCKS, 1)], min_val=0, max_val=E)
                with pool.Fori(first, end, PASS):
                    n = pool.snap(passes)
                    pool.wait_ge(ld_idx, n * 16 + 16)
                    for load in range(LOADS):
                        pool.wait_ge(p_used, n * LOADS + (load + 1))
                        pool.sem_inc(pool_turn, 1)
                        for j in range(load * PER_LOAD, (load + 1) * PER_LOAD):
                            pool.indirect_dma_start(
                                out=rows[:, j, :], out_offset=None, in_=table[:, :],
                                in_offset=bass.IndirectOffsetOnAxis(ap=idx[:, j:j + 1], axis=0)).then_inc(gathered[load], 16)
                    pool.reg_add(passes, passes, 1)

            gather(0)
            pool.wait_ge(v_max, 1)
            pool.partition_all_reduce(wmaxa[:, :], wmax[:, :], P, RMAX).then_inc(pool_max, 1)

            def block(c, q, par, ffns):
                b = c * CHUNK + q
                if not (isinstance(b, int) and b == BLOCKS - 1):
                    gather(b + 1)

            main(pool, block)

        @block_ctx.tensor
        def _(pe):
            first_credit(pe, ["p_t1", "p_agg", "p_t2", "p_h", "p_t3", "p_gu", "p_dn", "p_t4"])
            pe.sem_inc(p_used, LOADS)
            pe.wait_ge(pool_c, 3)

            for w in range(3):
                with pe.Fori(0, FT) as i:
                    pe.wait_ge(v_cmp, i + (w * FT + 1))
                    done(pe, a_tern, i + w * FT)
                    for g in range(KT):
                        to = tr_ps[:, g * P:(g + 1) * P]
                        pe.matmul(to, above[:, bass.ds(i * KT + g, 1), :].rearrange("p a k -> p (a k)"), ident[:, 0, :],
                                  start=True, stop=False)
                        mm = pe.matmul(to, below[:, bass.ds(i * KT + g, 1), :].rearrange("p a k -> p (a k)"), ident[:, 1, :],
                                       start=False, stop=True)
                    mm.then_inc(p_tern, 1)

            pe.wait_ge(ld_const, 80)
            pe.wait_ge(ld_bias, 64)
            done(pe, a_tern, 3 * FT)
            passes = pe.alloc_register("pe_passes")
            pe.reg_mov(passes, 0)

            def transpose4(source):
                for k in range(KT):
                    mm = pe.transpose(tr_ps[:, k * P:(k + 1) * P], source(k), identf[:, :])
                return mm

            def ffn(c, q, par, width):
                xhi = x1T[:, par, 0]
                xlo = x1T[:, par, 1]
                for f in QF[q]:
                    for w in range(2):
                        for g in range(KT):
                            s = f * 8 + w * 4 + g
                            if s < 4:
                                done(pe, v_dn, c * (KT * (FT - 1)))
                            elif g == 0:
                                done(pe, a_gu, c * (2 * FT) + (2 * f + w))
                            else:
                                done(pe, v_gu, c * (6 * FT) + (3 * (2 * f + w) - 3 + g))
                            to = f_ps[g][:, 0:width]
                            lhs = tern[:, w, f * KT + g, :]
                            pe.matmul(to, lhs, xhi[:, g, 0:width], start=True, stop=False)
                            pe.matmul(to, lhs, xlo[:, g, 0:width], start=False, stop=True).then_inc(p_gu, 1)
                for d in QD[q]:
                    for g in range(FT):
                        r = d * FT + g
                        if r < 4:
                            if r == 0:
                                done(pe, a_gu, c * (2 * FT) + 2 * FT)
                            done(pe, v_gu, c * (6 * FT) + (6 * FT - 3 + r) if r else c * (6 * FT) + 6 * FT - 3)
                        else:
                            pd, pg = divmod(r - 4, FT)
                            if pg == 0:
                                done(pe, a_dn, c * KT + (pd + 1))
                            else:
                                done(pe, v_dn, c * (KT * (FT - 1)) + (pd * (FT - 1) + pg))
                        if d == 0:
                            done(pe, v_lo, c * FT + (g + 1))
                        to = f_ps[r % 4][:, 0:width]
                        lhs = tern[:, 2, d * FT + g, :]
                        pe.matmul(to, lhs, hT[:, 0, g, 0:width], start=True, stop=False)
                        pe.matmul(to, lhs, hT[:, 1, g, 0:width], start=False, stop=True).then_inc(p_dn, 1)
                if q == 3:
                    done(pe, v_dn, c * (KT * (FT - 1)) + KT * (FT - 1))
                    for qq in range(width // P):
                        done(pe, v_out, c * CHUNK + qq)
                        transpose4(lambda k: yT[:, k, qq * P:(qq + 1) * P]).then_inc(p_t4, 1)

            def block(c, q, par, ffns):
                b = c * CHUNK + q
                done(pe, v_xs, b + 1)
                done(pe, v_lo1, b)
                done(pe, a_hi1, b)
                transpose4(lambda k: xs[:, k * P:(k + 1) * P]).then_inc(p_t1, 1)
                done(pe, a_ng, b)
                done(pe, v_inv, b)
                done(pe, v_x1, b)
                done(pe, v_lo, ((c - 1) * FT + F_AFTER[q - 1] if q else (c - 1) * FT) if not (isinstance(c, int) and c == 0) else 0)
                pe.matmul(agg_ps[:, 0:1], zeros[:, :], zeros[:, 0:1], start=True, stop=False, skip_group_check=True)
                pe.matmul(misc_ps[:, 0:1], zeros[:, :], zeros[:, 0:1], start=True, stop=False, skip_group_check=True)
                first = pe.value_load(rangei[0:1, bass.ds(b, 1)], min_val=0, max_val=E)
                end = pe.value_load(rangei[0:1, bass.ds(b + BLOCKS, 1)], min_val=0, max_val=E)
                with pe.Fori(first, end, PASS):
                    n = pe.snap(passes)
                    done(pe, v_hot, n + 1)
                    for load in range(LOADS):
                        pe.wait_ge(gathered[load], n * (16 * PER_LOAD) + 16 * PER_LOAD)
                        for j in range(load * PER_LOAD, (load + 1) * PER_LOAD):
                            pe.matmul(misc_ps[:, 0:1], hot[:, :, j], ones[:, 0:1], start=False, stop=False, skip_group_check=True)
                            for part in range(2):
                                mm = pe.matmul(agg_ps[:, :], hot[:, :, j], rows[:, j, part * D:(part + 1) * D],
                                               start=False, stop=False, skip_group_check=True)
                        mm.then_inc(p_used, 1)
                    pe.reg_add(passes, passes, 1)
                pe.matmul(agg_ps[:, 0:1], zeros[:, :], zeros[:, 0:1], start=False, stop=True, skip_group_check=True)
                pe.matmul(misc_ps[:, 0:1], zeros[:, :], zeros[:, 0:1], start=False, stop=True,
                          skip_group_check=True).then_inc(p_agg, 1)
                done(pe, a_xsT, b + 1)
                pe.matmul(h_ps[:, :], onesb[:, :], bparts[:, :], start=True, stop=False)
                for k in range(KT):
                    pe.matmul(h_ps[:, :], xsT[:, k, :], wself[:, k, :], start=False, stop=False)
                done(pe, a_ng, b + 1)
                transpose4(lambda k: ng[:, k * P:(k + 1) * P]).then_inc(p_t2, 1)
                done(pe, a_ngT, b + 1)
                for k in range(KT):
                    mm = pe.matmul(h_ps[:, :], ngT[:, k, :], wneigh[:, k, :], start=False, stop=(k == KT - 1))
                mm.then_inc(p_h, 1)
                for qq in ffns:
                    ffn(c - 1, qq, 1 - par, CW)
                done(pe, v_x1s, b + 1)
                if 3 in ffns:
                    done(pe, v_out, c * CHUNK)
                transpose4(lambda k: x1s[:, k * P:(k + 1) * P]).then_inc(p_t3, 1)

            main(pe, block)
            done(pe, v_lo1, BLOCKS)
            done(pe, a_hi1, BLOCKS)
            for q in range(CHUNK):
                ffn(FULL, q, FULL % 2, P)

        @block_ctx.scalar
        def _(act):
            first_credit(act, ["a_norm", "a_high", "a_tern", "a_xsT", "a_ng", "a_ngT", "a_y", "a_hi1",
                               "a_gu", "a_silu", "a_hi", "a_dn"])
            nbank = [agg_ps, h_ps, tr_ps, misc_ps]
            for g in range(GROUPS):
                act.wait_ge(v_stat, g + 1)
                if g >= 2:
                    act.wait_ge(st_t[g % 2], 16 * (g // 2))
                for t in range(GROUP):
                    i = g * GROUP + t
                    done(act, v_low, max(i - 3, 0))
                    act.activation(nbank[i % 4][:, :], xgroup[:, g % 2, t, :], ACT.Identity, bias=nmr_k[:, i:i + 1],
                                   scale=rstd_k[:, i:i + 1]).then_inc(a_norm, 1)
                    done(act, a_norm, i + 1)
                    act.activation(tstage[g % 2][:, t, 0:D], nbank[i % 4][:, :], ACT.Copy).then_inc(a_high, 1)
            for w in range(3):
                with act.Fori(0, FT) as i:
                    done(act, v_low, BLOCKS)
                    act.wait_ge(p_tern, i + (w * FT + 1))
                    act.activation(tern[:, w, bass.ds(i * KT, KT), :].rearrange("p g k -> p (g k)"), tr_ps[:, :],
                                   ACT.Copy).then_inc(a_tern, 1)
            act.wait_ge(ld_const, 80)
            act.wait_ge(v_scl, 1)

            def high_hidden(c, f, width):
                done(act, v_h, c * FT + (f + 1))
                act.activation(hT[:, 0, f, 0:width], misc_ps[:, 0:width], ACT.Copy).then_inc(a_hi, 1)

            def ffn(c, q, width):
                fs = QF[q]
                for f in fs:
                    for w in range(2):
                        act.wait_ge(p_gu, c * (8 * FT) + (f * 8 + w * 4 + 2))
                        if w == 1:
                            done(act, v_h, c * FT + (f - 1) if f >= 1 else c * FT)
                        act.activation(acc[:, w, f % 2, 0:width], f_ps[0][:, 0:width], ACT.Copy,
                                       scale=scl[:, w, f * KT:f * KT + 1]).then_inc(a_gu, 1)
                        if w == 0 and f > fs[0]:
                            high_hidden(c, f - 1, width)
                    done(act, v_gu, c * (6 * FT) + (6 * f + 3))
                    done(act, v_lo, c * FT + f)
                    act.activation(misc_ps[:, 0:width], acc[:, 0, f % 2, 0:width], ACT.Silu).then_inc(a_silu, 1)
                if len(fs):
                    high_hidden(c, fs[-1], width)
                for d in QD[q]:
                    act.wait_ge(p_dn, c * (KT * FT) + (d * FT + 2))
                    if d == 0:
                        done(act, p_t4, c * CHUNK)
                    act.activation(yT[:, d, 0:width], f_ps[(d * FT) % 4][:, 0:width], ACT.Copy,
                                   scale=scl[:, 2, d * FT:d * FT + 1]).then_inc(a_dn, 1)

            def block(c, q, par, ffns):
                b = c * CHUNK + q
                done(act, p_t1, b + 1)
                done(act, p_h, b)
                act.activation(xsT[:, :, :].rearrange("p k n -> p (k n)"), tr_ps[:, :], ACT.Copy).then_inc(a_xsT, 1)
                done(act, p_agg, b + 1)
                done(act, v_inv, b + 1)
                done(act, p_t2, b)
                act.activation(ng[:, :], agg_ps[:, :], ACT.Copy, scale=small[:, 1:2]).then_inc(a_ng, 1)
                done(act, p_t2, b + 1)
                act.activation(ngT[:, :, :].rearrange("p k n -> p (k n)"), tr_ps[:, :], ACT.Copy).then_inc(a_ngT, 1)
                done(act, v_t2, b + 1)
                act.activation(agg_ps[:, :], t2[:, :], ACT.Relu, scale=-1.0)
                act.activation(h_ps[:, :], t2[:, :], ACT.Relu).then_inc(a_y, 1)
                for qq in ffns:
                    ffn(c - 1, qq, CW)
                done(act, p_t3, b + 1)
                act.activation(x1T[:, par, 0, :, q * P:(q + 1) * P], tr_ps[:, :].rearrange("p (k n) -> p k n", k=KT),
                               ACT.Copy, scale=XSCALE).then_inc(a_hi1, 1)

            main(act, block)
            for q in range(CHUNK):
                ffn(FULL, q, P)

        @block_ctx.vector
        def _(dve):
            first_credit(dve, ["v_low", "v_xs", "v_xx", "v_dl", "v_hot", "v_inv", "v_t2", "v_x1", "v_x1s", "v_lo1",
                               "v_gu", "v_h", "v_lo", "v_dn", "v_out"])

            class Chain:

                def __init__(self, s, start=0):
                    self.s, self.n, self.start = s, 0, start

                def step(self, ins):
                    ins.then_inc(self.s, 1)
                    self.n += 1
                    dve.wait_ge(self.s, self.start + self.n)

            def rsqrt(chain, v, y, a, vh):
                chain.step(dve.tensor_scalar(a, v, EPS, None, ALU.add))
                dve.tensor_scalar(vh, a, 0.5, None, ALU.mult)
                chain.step(dve.tensor_scalar(y.bitcast(I32), a.bitcast(I32), 1, None, ALU.logical_shift_right))
                chain.step(dve.tensor_scalar(y.bitcast(I32), y.bitcast(I32), -1.0, RSQRT_GUESS, ALU.mult, ALU.add))
                for _ in range(3):
                    if y.shape[-1] == 1:
                        chain.step(dve.tensor_scalar(a, y, y, vh, ALU.mult, ALU.mult))
                    else:
                        chain.step(dve.tensor_tensor(a, y, y, ALU.mult))
                        chain.step(dve.tensor_tensor(a, a, vh, ALU.mult))
                    chain.step(dve.scalar_tensor_tensor(out=y, in0=a, scalar=1.5, in1=y, op0=ALU.subtract, op1=ALU.mult))

            pro = Chain(v_pro)
            dve.wait_ge(ld_dst, 16)
            pro.step(dve.tensor_copy(dst_f, dst_i))
            dve.sem_inc(v_dst, 1)
            seg3 = dst_f.rearrange("p (s e) -> p s e", e=SEG)
            dve.tensor_reduce(segs[0:EP, 0, :], seg3, AX.X, ALU.min)
            dve.tensor_reduce(segs[0:EP, 1, :], seg3, AX.X, ALU.max)
            dve.wait_ge(pool_c, 3)
            dve.tensor_copy(base[:, :], rangei[:, 0:BLOCKS])
            pro.step(dve.tensor_scalar(top[:, :], rangei[:, 0:BLOCKS], float(P - 1), None, ALU.add))
            dve.tensor_scalar(segs[:, 2, :], posi[:, :], -1.0, BIG, ALU.mult, ALU.add)
            pro.step(dve.tensor_scalar(segs[:, 3, :], posi[:, :], float(SEG), None, ALU.add))

            def over_blocks(v):
                return v[0:EP, None, :].broadcast_to((EP, BLOCKS, NSEG))

            def over_segs(v):
                return v[0:EP, :, None].broadcast_to((EP, BLOCKS, NSEG))

            dve.tensor_tensor(hit[0], over_blocks(segs[:, 0, :]), over_segs(top[:, :]), ALU.is_le)
            pro.step(dve.tensor_tensor(hit[1], over_blocks(segs[:, 1, :]), over_segs(base[:, :]), ALU.is_ge))
            pro.step(dve.tensor_tensor(hit[0], hit[0], hit[1], ALU.mult))
            dve.tensor_tensor(hit[1], hit[0], over_blocks(segs[:, 2, :]), ALU.mult)
            pro.step(dve.tensor_tensor(hit[2], hit[0], over_blocks(segs[:, 3, :]), ALU.mult))
            dve.tensor_reduce(ranges[0:EP, 0:BLOCKS], hit[1], AX.X, ALU.max)
            dve.tensor_reduce(ranges[0:EP, BLOCKS:2 * BLOCKS], hit[2], AX.X, ALU.max).then_inc(v_rng, 1)
            dve.wait_ge(ld_bias, 16)
            for i in range(3):
                pro.step(dve.tensor_copy(browb[:, i, :], brow[:, i, :]))
                if i < 2:
                    pro.step(dve.tensor_tensor(brow[:, i + 1, :], brow[:, i, :], browb[:, i, :], ALU.subtract))
            dve.sem_inc(v_bias, 1)
            dve.wait_ge(pool_rng, 1)
            pro.step(dve.tensor_scalar(rangem[:, 0:BLOCKS], rangem[:, 0:BLOCKS], -1.0, BIG, ALU.mult, ALU.add))
            pro.step(dve.tensor_scalar(rangem[:, 0:BLOCKS], rangem[:, 0:BLOCKS], float(E), None, ALU.min))
            dve.tensor_copy(rangei[:, :], rangem[:, :]).then_inc(v_rngi, 1)

            loaded = [0, 0]
            nbank = [agg_ps, h_ps, tr_ps, misc_ps]

            def group_stats(g):
                loaded[g % 2] += 32 if g == GROUPS - 1 else 16
                dve.wait_ge(ld_xg[g % 2], loaded[g % 2])
                lo, hi = g * GROUP, (g + 1) * GROUP
                for t in range(GROUP):
                    ins = dve.bn_stats(stats6[:, t, :], xgroup[:, g % 2, t, :])
                pro.step(ins)
                for t in range(GROUP):
                    ins = dve.bn_aggr(mv[:, lo + t, :], stats6[:, t, :])
                pro.step(ins)
                rsqrt(pro, mv[:, lo:hi, 1], rstd[:, lo:hi], tmp[:, 0, :], tmp[:, 1, :])
                dve.tensor_scalar(rstd_k[:, lo:hi], rstd[:, lo:hi], XSCALE, None, ALU.mult)
                dve.tensor_scalar(one_r[:, lo:hi], rstd[:, lo:hi], 1.0, None, ALU.add)
                pro.step(dve.scalar_tensor_tensor(out=nmr[:, lo:hi], in0=mv[:, lo:hi, 0], scalar=-1.0,
                                                  in1=rstd[:, lo:hi], op0=ALU.mult, op1=ALU.mult))
                dve.tensor_scalar(nmr_k[:, lo:hi], nmr[:, lo:hi], XSCALE, None, ALU.mult).then_inc(v_stat, 1)

            def group_low(g):
                for t in range(GROUP):
                    i = g * GROUP + t
                    done(dve, a_high, i + 1)
                    dve.tensor_tensor(tstage[g % 2][:, t, D:2 * D], nbank[i % 4][:, :], tstage[g % 2][:, t, 0:D],
                                      ALU.subtract).then_inc(v_low, 1)

            group_stats(0)
            for g in range(GROUPS):
                if g + 1 < GROUPS:
                    group_stats(g + 1)
                group_low(g)

            passes = dve.alloc_register("dve_passes")
            dve.reg_mov(passes, 0)

            def one_hot(b):
                first = dve.value_load(rangei[0:1, bass.ds(b, 1)], min_val=0, max_val=E)
                end = dve.value_load(rangei[0:1, bass.ds(b + BLOCKS, 1)], min_val=0, max_val=E)
                with dve.Fori(first, end, PASS):
                    n = dve.snap(passes)
                    dve.wait_ge(ld_dv, n * 16 + 16)
                    done(dve, v_hot, n)
                    dve.tensor_scalar(dstl[:, :], dstv[:, :], base[:, bass.ds(b, 1)], None, ALU.subtract).then_inc(v_dl, 1)
                    done(dve, v_dl, n + 1)
                    dve.wait_ge(p_used, n * LOADS + LOADS)
                    dve.tensor_tensor(hot[:, :, :], dstl[:, None, :].broadcast_to((P, P, STEPS)), node_j[:, :, :],
                                      ALU.is_equal).then_inc(v_hot, 1)
                    dve.reg_add(passes, passes, 1)

            def own_rows(b, q):
                if isinstance(b, int):
                    turns = (b // 2 + 1) * 16
                else:
                    turns = (b - q % 2) * 8 + 16
                dve.wait_ge(ld_x[q % 2], turns)
                done(dve, p_t1, b)
                dve.tensor_scalar(xs[:, :], xin[:, q % 2, :], rstd[:, bass.ds(b, 1)], nmr[:, bass.ds(b, 1)],
                                  ALU.mult, ALU.add).then_inc(v_xs, 1)
                dve.tensor_scalar(xx[:, :], xin[:, q % 2, :], one_r[:, bass.ds(b, 1)], nmr[:, bass.ds(b, 1)],
                                  ALU.mult, ALU.add).then_inc(v_xx, 1)

            one_hot(0)
            own_rows(0, 0)

            for w in range(3):
                dve.wait_ge(ld_w[w], 16)
                pro.step(dve.tensor_reduce(scl[:, w, :], wstage, AX.X, ALU.add, apply_absolute_value=True))
                pro.step(dve.tensor_scalar(scl[:, w, :], scl[:, w, :], 1.0 / P, EPS, ALU.mult, ALU.add))
                dve.tensor_scalar(half[:, 0, :], scl[:, w, :], 0.5, None, ALU.mult)
                pro.step(dve.tensor_scalar(half[:, 1, :], scl[:, w, :], -0.5, None, ALU.mult))
                if w == 0:
                    dve.wait_ge(st_t[0], 16 * ((GROUPS + 1) // 2) + 16 * (GROUPS % 2))
                    dve.wait_ge(st_t[1], 16 * (GROUPS // 2) + 16 * ((GROUPS + 1) % 2))
                else:
                    dve.wait_ge(p_tern, w * FT)
                with dve.Fori(0, FT) as i:
                    for g in range(KT):
                        j = bass.ds(i * KT + g, 1)
                        dve.tensor_scalar(above[:, j, :], wstage[:, j, :], half[:, 0, j], None, ALU.is_gt)
                        ins = dve.tensor_scalar(below[:, j, :], wstage[:, j, :], half[:, 1, j], None, ALU.is_lt)
                    ins.then_inc(v_cmp, 1)
            dve.tensor_reduce(wmax[:, 0:1], scl[:, 0, :], AX.X, ALU.max)
            dve.tensor_reduce(wmax[:, 1:2], scl[:, 1, :], AX.X, ALU.max).then_inc(v_max, 1)
            dve.wait_ge(pool_max, 1)
            pro.step(dve.tensor_scalar(hsc[:, 0:1], wmaxa[:, 0:1], wmaxa[:, 1:2], float(D * D) / 2.0 ** 15, ALU.mult, ALU.mult))
            pro.step(dve.reciprocal(hsc[:, 1:2], hsc[:, 0:1]))
            pro.step(dve.tensor_scalar(hsc[:, 2:3].bitcast(I32), hsc[:, 1:2].bitcast(I32), EXPONENT_BITS, None, ALU.bitwise_and))
            pro.step(dve.tensor_scalar(hsc[:, 3:4].bitcast(I32), hsc[:, 2:3].bitcast(I32), -1.0, TWICE_BIAS_BITS, ALU.mult, ALU.add))
            dve.tensor_scalar(scl[:, 0, :], scl[:, 0, :], 1.0 / XSCALE, None, ALU.mult)
            dve.tensor_scalar(scl[:, 1, :], scl[:, 1, :], hsc[:, 2:3], 1.0 / XSCALE, ALU.mult, ALU.mult)
            pro.step(dve.tensor_scalar(scl[:, 2, :], scl[:, 2, :], hsc[:, 3:4], None, ALU.mult))
            dve.sem_inc(v_scl, 1)
            dve.wait_ge(ld_const, 80)
            pro.step(dve.tensor_scalar(neg_alpha[:, :], alpha_c[:, :], -1.0, None, ALU.mult))

            def add_groups(c, f, w, width):
                for g in range(1, KT):
                    dve.wait_ge(p_gu, c * (8 * FT) + (f * 8 + w * 4 + g + 2))
                    if g == 1:
                        done(dve, a_gu, c * (2 * FT) + (2 * f + w + 1))
                    else:
                        done(dve, v_gu, c * (6 * FT) + (3 * (2 * f + w) + g - 1))
                    a = acc[:, w, f % 2, 0:width]
                    dve.scalar_tensor_tensor(out=a, in0=f_ps[g][:, 0:width], scalar=scl[:, w, f * KT + g:f * KT + g + 1],
                                             in1=a, op0=ALU.mult, op1=ALU.add).then_inc(v_gu, 1)

            def low_hidden(c, f, width):
                done(dve, a_hi, c * FT + (f + 1))
                dve.tensor_tensor(hT[:, 1, f, 0:width], misc_ps[:, 0:width], hT[:, 0, f, 0:width],
                                  ALU.subtract).then_inc(v_lo, 1)

            def ffn(c, q, par, width):
                fs = QF[q]
                for f in fs:
                    add_groups(c, f, 0, width)
                    if f > fs[0]:
                        low_hidden(c, f - 1, width)
                    elif f == 0:
                        done(dve, p_dn, c * (KT * FT))
                    add_groups(c, f, 1, width)
                    done(dve, a_silu, c * FT + (f + 1))
                    done(dve, v_gu, c * (6 * FT) + (6 * f + 6))
                    dve.tensor_tensor(misc_ps[:, 0:width], misc_ps[:, 0:width], acc[:, 1, f % 2, 0:width],
                                      ALU.mult).then_inc(v_h, 1)
                if len(fs):
                    low_hidden(c, fs[-1], width)
                for d in QD[q]:
                    for g in range(1, FT):
                        dve.wait_ge(p_dn, c * (KT * FT) + (d * FT + g + 2))
                        if g == 1:
                            done(dve, a_dn, c * KT + (d + 1))
                        else:
                            done(dve, v_dn, c * (KT * (FT - 1)) + (d * (FT - 1) + g - 1))
                        y = yT[:, d, 0:width]
                        dve.scalar_tensor_tensor(out=y, in0=f_ps[(d * FT + g) % 4][:, 0:width],
                                                 scalar=scl[:, 2, d * FT + g:d * FT + g + 1], in1=y,
                                                 op0=ALU.mult, op1=ALU.add).then_inc(v_dn, 1)
                if q == 3:
                    for qq in range(width // P):
                        done(dve, p_t4, c * CHUNK + (qq + 1))
                        if qq >= 2:
                            done(dve, stored, c * CHUNK + (qq - 1))
                        else:
                            done(dve, stored, c * CHUNK)
                        dve.tensor_tensor(outb[:, qq % 2, :], tr_ps[:, :], x1[:, par, qq, :], ALU.add).then_inc(v_out, 1)

            PER_BLOCK = [0]

            def block(c, q, par, ffns):
                b = c * CHUNK + q
                chain = Chain(v_chain, b * CHAIN_STEPS)
                done(dve, p_agg, b + 1)
                done(dve, a_ng, b)
                chain.step(dve.tensor_scalar(small[:, 0:1], misc_ps[:, 0:1], 1.0, XSCALE, ALU.max, ALU.mult))
                dve.reciprocal(small[:, 1:2], small[:, 0:1]).then_inc(v_inv, 1)
                done(dve, p_h, b + 1)
                chain.step(dve.bn_stats(st6[:, :], h_ps[:, :]))
                dve.sem_inc(dve_turn, 1)
                chain.step(dve.bn_aggr(small[:, 2:4], st6[:, :]))
                rsqrt(chain, small[:, 3:4], small[:, 4:5], small[:, 5:6], small[:, 6:7])
                chain.step(dve.scalar_tensor_tensor(out=h_ps[:, :], in0=h_ps[:, :], scalar=small[:, 2:3],
                                                    in1=gamma_b[:, :], op0=ALU.subtract, op1=ALU.mult))
                done(dve, a_y, b)
                dve.scalar_tensor_tensor(out=t2[:, :], in0=h_ps[:, :], scalar=small[:, 4:5], in1=beta_b[:, :],
                                         op0=ALU.mult, op1=ALU.add).then_inc(v_t2, 1)
                done(dve, a_y, b + 1)
                chain.step(dve.scalar_tensor_tensor(out=xx[:, :], in0=agg_ps[:, :], scalar=neg_alpha[:, 0:1],
                                                    in1=xx[:, :], op0=ALU.mult, op1=ALU.add))
                dve.tensor_tensor(x1[:, par, q, :], h_ps[:, :], xx[:, :], ALU.add).then_inc(v_x1, 1)
                done(dve, v_x1, b + 1)
                chain.step(dve.bn_stats(st6[:, :], x1[:, par, q, :]))
                dve.sem_inc(dve_turn, 1)
                chain.step(dve.bn_aggr(small[:, 8:10], st6[:, :]))
                rsqrt(chain, small[:, 9:10], small[:, 10:11], small[:, 11:12], small[:, 12:13])
                done(dve, p_t3, b)
                dve.tensor_scalar(x1s[:, :], x1[:, par, q, :], small[:, 8:9], small[:, 10:11], ALU.subtract,
                                  ALU.mult).then_inc(v_x1s, 1)
                assert chain.n == CHAIN_STEPS, chain.n
                for qq in ffns:
                    ffn(c - 1, qq, 1 - par, CW)
                if not (isinstance(b, int) and b == BLOCKS - 1):
                    one_hot(b + 1)
                    own_rows(b + 1, q + 1)
                done(dve, p_t3, b + 1)
                done(dve, a_hi1, b + 1)
                dve.scalar_tensor_tensor(out=x1T[:, par, 1, :, q * P:(q + 1) * P],
                                         in0=tr_ps[:, :].rearrange("p (k n) -> p k n", k=KT), scalar=XSCALE,
                                         in1=x1T[:, par, 0, :, q * P:(q + 1) * P], op0=ALU.mult,
                                         op1=ALU.subtract).then_inc(v_lo1, 1)

            main(dve, block)
            for q in range(CHUNK):
                ffn(FULL, q, FULL % 2, P)


CHAIN_STEPS = 1 + 2 * (2 + 9) + 2

_INS = ["x", "src", "dst", "L0_gnn_W_self", "L0_gnn_b_self", "L0_gnn_W_neigh", "L0_gnn_gamma", "L0_gnn_beta",
        "L0_gnn_alpha", "L0_ffn_w_gate", "L0_ffn_w_up", "L0_ffn_w_down"]


def kernel(**inputs):
    import concourse.bacc as bacc
    from concourse.bass_utils import run_bass_kernel_spmd

    nc = bacc.Bacc("TRN2", target_bir_lowering=False, num_devices=1)
    arrays, args = {}, []
    for name in _INS:
        a = np.ascontiguousarray(inputs[name])
        if a.ndim == 0:
            a = a.reshape(1)
        arrays[f"in_{name}"] = a
        args.append(nc.dram_tensor(f"in_{name}", a.shape, mybir.dt.from_np(a.dtype), kind="ExternalInput").ap())
    shape = np.shape(inputs["x"])
    args.append(nc.dram_tensor("out_nodes", shape, F32, kind="ExternalOutput").ap())
    build(nc, *args)
    r = run_bass_kernel_spmd(nc, [arrays], core_ids=[0])
    return r.results[0]["out_nodes"]
```

```python
from contextlib import ExitStack

import numpy as np

import concourse.bass as bass
from concourse import mybir

ALU = mybir.AluOpType
ACT = mybir.ActivationFunctionType
F32 = mybir.dt.float32
F16 = mybir.dt.float16
BF16 = mybir.dt.bfloat16
I32 = mybir.dt.int32
AX = mybir.AxisListType
RMAX = bass.bass_isa.ReduceOp.max

P = 128
EPS = 1e-5
XSCALE = 1024.0
RSQRT_GUESS = float(0x5F1FFFF9 - (1 << 31))
RSQRT_FIRST, RSQRT_GAIN = 2.38924456, 0.703952253
EXPONENT_BITS = 0x7F800000
TWICE_BIAS_BITS = float(0x7F000000)
STEPS = 18
PER_LOAD = 3
LOADS = STEPS // PER_LOAD
BIG = float(1 << 17)


def build(nc, x, src, dst, W_self, b_self, W_neigh, gamma, beta, alpha, w_gate, w_up, w_down, out):
    N, D = x.shape
    E = src.shape[0]
    FFN = w_gate.shape[0]
    KT = D // P
    FT = FFN // P
    NG = FT * KT
    BLOCKS = -(-N // P)
    LAST = N - (BLOCKS - 1) * P
    CHUNK = 4
    CW = CHUNK * P
    FULL = (BLOCKS - 1) // CHUNK
    assert BLOCKS == FULL * CHUNK + 1 and FULL % 2 == 0 and D == CW
    PASS = STEPS * P
    EP = 125
    SEG = 17
    EROW = E // EP
    NSEG = EROW // SEG
    assert EP * NSEG * SEG == E
    GROUP = 7
    GROUPS = BLOCKS // GROUP
    assert GROUP * GROUPS == BLOCKS

    table = nc.dram_tensor("node_table", (N, 2 * D), F16, kind="Internal").ap()
    src_pad = nc.dram_tensor("src_pad", (E + PASS,), I32, kind="Internal").ap()
    dst_pad = nc.dram_tensor("dst_pad", (E + PASS,), F32, kind="Internal").ap()

    with ExitStack() as ctx:
        def sb(name, shape, dt):
            return ctx.enter_context(nc.sbuf_tensor(name, shape, dt))

        def bank(name):
            return ctx.enter_context(nc.psum_tensor(name, [P, 512], F32))

        sems = {}

        def sem(name):
            sems[name] = ctx.enter_context(nc.semaphore(name))
            return sems[name]

        rows = sb("rows", [P, STEPS, 2 * D], F16)
        wself = sb("wself", [P, KT, D], F32)
        wneigh = sb("wneigh", [P, KT, D], F32)
        tern = sb("tern", [P, 3, NG, P], F16)
        x1 = sb("x1", [P, 2, CHUNK, D], F32)
        x1T = sb("x1T", [P, 2, 2, KT, CW], F16)
        hT = sb("hT", [P, 2, FT, CW], F16)
        yT = sb("yT", [P, KT, CW], F32)
        acc = sb("acc", [P, 2, 2, CW], F32)
        xin = sb("xin", [P, 2, D], F32)
        xs = sb("xs", [P, D], F32)
        xx = sb("xx", [P, 2, D], F32)
        neg = sb("neg", [P, D], F32)
        t2 = sb("t2", [P, D], F32)
        x1s = sb("x1s", [P, D], F32)
        outb = sb("outb", [P, 2, D], F32)
        xsT = sb("xsT", [P, KT, P], F32)
        ng = sb("ng", [P, D], F32)
        ngT = sb("ngT", [P, KT, P], F32)
        gamma_b = sb("gamma_b", [P, D], F32)
        beta_b = sb("beta_b", [P, D], F32)
        hot = sb("hot", [P, P, STEPS], F16)
        node_j = sb("node_j", [P, P, STEPS], F16)
        idx = sb("idx", [P, STEPS], I32)
        dstv = sb("dstv", [P, STEPS], F32)
        dstl = sb("dstl", [P, STEPS], F16)
        identf = sb("identf", [P, P], F32)
        ident = sb("ident", [P, 2, P], F16)
        zeros = sb("zeros", [P, P], F16)
        ones = sb("ones", [P, P], F16)
        bparts = sb("bparts", [3, D], BF16)
        onesb = sb("onesb", [3, P], BF16)
        alpha_c = sb("alpha_c", [P, 1], F32)
        neg_alpha = sb("neg_alpha", [P, 1], F32)
        base = sb("base", [P, BLOCKS], F32)
        top = sb("top", [P, BLOCKS], F32)
        stats6 = sb("stats6", [P, GROUP, 6], F32)
        mv = sb("mv", [P, BLOCKS, 2], F32)
        rstd = sb("rstd", [P, BLOCKS], F32)
        nmr = sb("nmr", [P, BLOCKS], F32)
        rstd_k = sb("rstd_k", [P, BLOCKS], F32)
        nmr_k = sb("nmr_k", [P, BLOCKS], F32)
        one_r = sb("one_r", [P, BLOCKS], F32)
        tmp = sb("tmp", [P, 4, GROUP], F32)
        small = sb("small", [P, 32], F32)
        st6 = sb("st6", [P, 6], F32)
        segs = sb("segs", [P, 4, NSEG], F32)
        posi = sb("posi", [P, NSEG], I32)
        ranges = sb("ranges", [P, 2 * BLOCKS], F32)
        rangem = sb("rangem", [P, 2 * BLOCKS], F32)
        rangei = sb("rangei", [P, 2 * BLOCKS], I32)
        padi = sb("padi", [P, STEPS], I32)
        padf = sb("padf", [P, STEPS], F32)
        scl = sb("scl", [P, 3, NG], F32)
        half = sb("half", [P, 2, NG], F32)
        wmax = sb("wmax", [P, 2], F32)
        wmaxa = sb("wmaxa", [P, 2], F32)
        hsc = sb("hsc", [P, 4], F32)

        agg_ps = bank("agg_ps")
        h_ps = bank("h_ps")
        tr_ps = bank("tr_ps")
        misc_ps = bank("misc_ps")
        f_ps = [bank(f"f_ps{i}") for i in range(4)]

        xgroup = rows[:, :, :].rearrange("p a b -> p (a b)").bitcast(F32)[:, 0:2 * GROUP * D].rearrange(
            "p (g t d) -> p g t d", g=2, t=GROUP)
        tstage = [x1[:, :, :, :].rearrange("p a b c -> p (a b c)").bitcast(F16)[:, 0:GROUP * 2 * D].rearrange(
            "p (t d) -> p t d", t=GROUP),
            x1T[:, :, :, :, :].rearrange("p a b c d -> p (a b c d)")[:, 0:GROUP * 2 * D].rearrange(
            "p (t d) -> p t d", t=GROUP)]
        wstage = hT[:, :, :, :].rearrange("p a b c -> p (a b c)").bitcast(F32).rearrange(
            "p (g k) -> p g k", g=NG)
        above = x1[:, :, :, :].rearrange("p a b c -> p (a b c)").bitcast(F16)[:, 0:NG * P].rearrange(
            "p (g k) -> p g k", g=NG)
        below = x1T[:, :, :, :, :].rearrange("p a b c d -> p (a b c d)")[:, 0:NG * P].rearrange(
            "p (g k) -> p g k", g=NG)
        tern32 = tern[:, :, :, :].rearrange("p w g k -> p w (g k)").bitcast(F32)
        hit = [tern32[0:EP, w, 0:BLOCKS * NSEG].rearrange("p (b s) -> p b s", b=BLOCKS) for w in range(3)]
        yflat = yT[:, :, :].rearrange("p a b -> p (a b)")
        dst_i = yflat[0:EP, 0:EROW].bitcast(I32)
        dst_f = yflat[0:EP, EROW:2 * EROW]

        brow = acc[0:1, :, :, :].rearrange("p a b c -> p (a b) c")
        browb = outb[0:1, :, :].rearrange("p a b -> p (a b)").bitcast(BF16)[:, 0:3 * D].rearrange("p (i d) -> p i d", i=3)

        ld_dst, ld_const, ld_bias, ld_pads = sem("ld_dst"), sem("ld_const"), sem("ld_bias"), sem("ld_pads")
        ld_w = [sem(f"ld_w{w}") for w in range(3)]
        ld_xg = [sem(f"ld_xg{i}") for i in range(2)]
        st_t = [sem(f"st_t{i}") for i in range(2)]
        ld_x = [sem(f"ld_x{i}") for i in range(2)]
        ld_idx, ld_dv = sem("ld_idx"), sem("ld_dv")
        gathered = [sem(f"gathered{i}") for i in range(LOADS)]
        st_out = sem("st_out")
        pool_c, pool_rng, pool_max = sem("pool_c"), sem("pool_rng"), sem("pool_max")
        v_pro, v_dst, v_rng, v_rngi, v_bias = sem("v_pro"), sem("v_dst"), sem("v_rng"), sem("v_rngi"), sem("v_bias")
        v_stat, v_low, v_cmp, v_max, v_scl = sem("v_stat"), sem("v_low"), sem("v_cmp"), sem("v_max"), sem("v_scl")
        a_norm, a_high, p_tern, a_tern = sem("a_norm"), sem("a_high"), sem("p_tern"), sem("a_tern")
        v_dl, p_used, v_hot, p_agg, v_deg, v_inv = (sem(n) for n in ("v_dl", "p_used", "v_hot", "p_agg", "v_deg", "v_inv"))
        a_xs, a_xx, p_t1, a_xsT, a_ng, p_t2, a_ngT, p_h = (
            sem(n) for n in ("a_xs", "a_xx", "p_t1", "a_xsT", "a_ng", "p_t2", "a_ngT", "p_h"))
        v_chain, v_t2, a_y, v_x1, v_n1, a_x1s, p_t3, a_hi1, v_lo1 = (
            sem(n) for n in ("v_chain", "v_t2", "a_y", "v_x1", "v_n1", "a_x1s", "p_t3", "a_hi1", "v_lo1"))
        p_up, p_dn, p_t4, a_up, a_dn, v_up, v_dn = (
            sem(n) for n in ("p_up", "p_dn", "p_t4", "a_up", "a_dn", "v_up", "v_dn"))
        a_silu, v_h, a_hi, v_lo, v_out, stored = (
            sem(n) for n in ("a_silu", "v_h", "a_hi", "v_lo", "v_out", "stored"))
        sp_turn, pool_turn, dve_turn = sem("sp_turn"), sem("pool_turn"), sem("dve_turn")

        def done(eng, s, n):
            eng.wait_ge(s, n + 1)

        def first_credit(eng, names):
            for name in names:
                eng.sem_inc(sems[name], 1)

        UP_STEPS = FT * KT * 2
        DOWN_STEPS = KT * FT
        ALL = UP_STEPS + DOWN_STEPS
        QUARTER = ALL // CHUNK
        LATE = 18
        IN_SUM = 14
        BY_OWN = (IN_SUM, IN_SUM, IN_SUM + 1, IN_SUM + 2, LATE)
        assert ALL % CHUNK == 0 and UP_STEPS % 4 == 0

        def place(s):
            if s < UP_STEPS:
                return ("up", s // (2 * KT), s // 2 % KT, s % 2)
            s -= UP_STEPS
            return ("down", s // (2 * FT), s // 2 % FT, s % 2)

        V_UP, V_DOWN, A_UP, A_DOWN = 2 * (KT - 1) * FT, (FT - 1) * KT, 2 * FT, KT

        def nth_v_up(f, g, w):
            return f * 2 * (KT - 1) + (g - 1) * 2 + w + 1

        def nth_v_down(pair, g, e):
            return pair * 2 * (FT - 1) + (g - 1) * 2 + e + 1

        NONE = (0, 0, range(0))

        def beside(c, q, par):
            at = QUARTER * ((q - 1) % CHUNK)
            late = range(at + QUARTER - LATE, at + QUARTER)
            first = (c - 2, par, late) if q == 0 else (c - 1, 1 - par, late)
            second = (c - 1, 1 - par, range(QUARTER * q, QUARTER * (q + 1) - LATE))
            return first, second

        def main(eng, block):
            for q in range(CHUNK):
                block(0, q, 0, NONE, NONE)
            for q in range(CHUNK):
                first, second = beside(1, q, 1)
                block(1, q, 1, first if q else NONE, second)
            with eng.Fori(0, (FULL - 4) // 2) as u:
                for h in range(2):
                    for q in range(CHUNK):
                        block(u * 2 + (2 + h), q, h, *beside(u * 2 + (2 + h), q, h))
            for c in range(FULL - 2, FULL):
                for q in range(CHUNK):
                    block(c, q, c % 2, *beside(c, q, c % 2))
            block(FULL, 0, 0, *beside(FULL, 0, 0))

        def number(c, q):
            b = c * CHUNK + q
            return b, isinstance(b, int) and b == BLOCKS - 1

        assert CHUNK == 4
        TO_MEAN, TO_OWN, TO_SLOPE = 4, 6, 7
        TO_LAST = 64

        block_ctx = ctx.enter_context(nc.Block())

        @block_ctx.sync
        def _(sp):
            first_credit(sp, ["stored"])
            sp.dma_start(dst_i, dst.rearrange("(p e) -> p e", p=EP)).then_inc(ld_dst, 16)

            def load_group(g):
                if g >= 2:
                    done(sp, a_norm, GROUP * (g - 1))
                    sp.wait_ge(v_stat, g - 1)
                if g < GROUPS - 1:
                    sp.dma_start(xgroup[:, g % 2], x[g * GROUP * P:(g + 1) * GROUP * P, :].rearrange(
                        "(t p) d -> p t d", p=P)).then_inc(ld_xg[g % 2], 16)
                else:
                    r0 = g * GROUP * P
                    sp.dma_start(xgroup[:, g % 2, 0:GROUP - 1], x[r0:r0 + (GROUP - 1) * P, :].rearrange(
                        "(t p) d -> p t d", p=P)).then_inc(ld_xg[g % 2], 16)
                    sp.dma_start(xgroup[0:LAST, g % 2, GROUP - 1], x[N - LAST:N, :]).then_inc(ld_xg[g % 2], 16)

            load_group(0)
            load_group(1)
            sp.dma_start(src_pad[0:E].rearrange("(p e) -> p e", p=EP), src.rearrange("(p e) -> p e", p=EP)).then_inc(ld_pads, 16)
            sp.wait_ge(pool_c, 1)
            sp.dma_start(src_pad[E:E + PASS].rearrange("(p e) -> p e", p=P), padi[:, :]).then_inc(ld_pads, 16)
            sp.dma_start(dst_pad[E:E + PASS].rearrange("(p e) -> p e", p=P), padf[:, :]).then_inc(ld_pads, 16)
            sp.wait_ge(v_dst, 1)
            sp.dma_start(dst_pad[0:E].rearrange("(p e) -> p e", p=EP), dst_f).then_inc(ld_pads, 16)
            sp.dma_start(brow[:, 0, :], b_self.rearrange("(a d) -> a d", a=1)).then_inc(ld_bias, 16)
            load_group(2)
            sp.dma_start(gamma_b[:, :], gamma.rearrange("(a d) -> a d", a=1).broadcast_to((P, D))).then_inc(ld_const, 16)
            sp.dma_start(beta_b[:, :], beta.rearrange("(a d) -> a d", a=1).broadcast_to((P, D))).then_inc(ld_const, 16)
            sp.dma_start(alpha_c[:, :], alpha.rearrange("(a d) -> a d", a=1).broadcast_to((P, 1))).then_inc(ld_const, 16)
            sp.dma_start(wself[:, :, :], W_self.rearrange("(k p) n -> p k n", p=P)).then_inc(ld_const, 16)
            sp.dma_start(wneigh[:, :, :], W_neigh.rearrange("(k p) n -> p k n", p=P)).then_inc(ld_const, 16)
            sp.wait_ge(v_bias, 1)
            for i in range(3):
                sp.dma_start(bparts[i:i + 1, :], browb[:, i, :]).then_inc(ld_bias, 16)
            sp.dma_start(wstage, w_gate.rearrange("(i p) (g k) -> p i g k", p=P, k=P)).then_inc(ld_w[0], 16)
            for g in range(GROUPS):
                if g + 3 < GROUPS:
                    load_group(g + 3)
                done(sp, v_low, GROUP * (g + 1))
                if g < GROUPS - 1:
                    sp.dma_start(table[g * GROUP * P:(g + 1) * GROUP * P, :].rearrange("(t p) d -> p t d", p=P),
                                 tstage[g % 2]).then_inc(st_t[g % 2], 16)
                else:
                    r0 = g * GROUP * P
                    sp.dma_start(table[r0:r0 + (GROUP - 1) * P, :].rearrange("(t p) d -> p t d", p=P),
                                 tstage[g % 2][:, 0:GROUP - 1]).then_inc(st_t[g % 2], 16)
                    sp.dma_start(table[N - LAST:N, :], tstage[g % 2][0:LAST, GROUP - 1]).then_inc(st_t[g % 2], 16)
            sp.wait_ge(ld_pads, 64)
            sp.wait_ge(v_rngi, 1)
            passes = sp.alloc_register("sp_passes")
            sp.reg_mov(passes, 0)

            def edges_range(b):
                return (sp.value_load(rangei[0:1, bass.ds(b, 1)], min_val=0, max_val=E),
                        sp.value_load(rangei[0:1, bass.ds(b + BLOCKS, 1)], min_val=0, max_val=E))

            def load_pass(at):
                n = sp.snap(passes)
                sp.wait_ge(p_used, n * LOADS + LOADS)
                sp.sem_inc(sp_turn, 1)
                done(sp, v_dl, n)
                sp.sem_inc(sp_turn, 1)
                sp.dma_start(idx[:, :], src_pad[bass.ds(at, PASS)].rearrange("(p e) -> p e", p=P)).then_inc(ld_idx, 16)
                sp.dma_start(dstv[:, :], dst_pad[bass.ds(at, PASS)].rearrange("(p e) -> p e", p=P)).then_inc(ld_dv, 16)
                sp.reg_add(passes, passes, 1)

            def load_first_pass(b):
                load_pass(edges_range(b)[0])

            def load_more_passes(b):
                first, end = edges_range(b)
                with sp.If(end > first + PASS):
                    with sp.Fori(first + PASS, end, PASS) as at:
                        load_pass(at)

            def load_x(b, q):
                last = isinstance(b, int) and b == BLOCKS - 1
                row = b * P if isinstance(b, int) else sp.snap(b * P)
                done(sp, a_xx, max(b - 1, 0) if isinstance(b, int) else b - 1)
                if last:
                    sp.dma_start(xin[0:LAST, q % 2], x[N - LAST:N, :]).then_inc(ld_x[q % 2], 16)
                else:
                    sp.dma_start(xin[:, q % 2], x[bass.ds(row, P), :]).then_inc(ld_x[q % 2], 16)

            load_x(0, 0)
            load_first_pass(0)
            load_more_passes(0)

            def store_out(c, q, rows_):
                row = (c * CHUNK + q) * P if isinstance(c, int) else sp.snap((c * CHUNK + q) * P)
                done(sp, v_out, c * CHUNK + q + 1)
                sp.dma_start(out[bass.ds(row, rows_), :], outb[0:rows_, q % 2]).then_inc(st_out, 16)
                sp.wait_ge(st_out, c * (16 * CHUNK) + (16 * q + 16))
                sp.sem_inc(stored, 1)

            def block(c, q, par, first, second):
                b, last = number(c, q)
                if not last:
                    load_x(b + 1, q + 1)
                    load_first_pass(b + 1)
                if q == 0 and len(first[2]):
                    for t in range(CHUNK):
                        store_out(first[0], t, P)
                if not last:
                    load_more_passes(b + 1)

            sp.wait_ge(v_cmp, FT)
            sp.dma_start(wstage, w_up.rearrange("(i p) (g k) -> p i g k", p=P, k=P)).then_inc(ld_w[1], 16)
            sp.wait_ge(v_cmp, 2 * FT)
            sp.dma_start(wstage, w_down.rearrange("(i p) (g k) -> p i g k", p=P, k=P)).then_inc(ld_w[2], 16)
            main(sp, block)
            for t in range(CHUNK):
                store_out(FULL - 1, t, P)
            store_out(FULL, 0, LAST)

        @block_ctx.gpsimd
        def _(pool):
            pool.memset(padi[:, :], 0)
            pool.memset(padf[:, :], -1.0).then_inc(pool_c, 1)
            pool.memset(ones[:, :], 1.0)
            pool.memset(onesb[:, :], 1.0)
            pool.memset(zeros[:, :], 0.0)
            pool.memset(xin[:, :, :], 0.0)
            pool.memset(ranges[:, :], 0.0)
            pool.memset(identf[:, :], 0.0)
            pool.memset(ident[:, :, :], 0.0).then_inc(pool_c, 1)
            pool.iota(padi_scratch := rangei[:, 0:BLOCKS], pattern=[[P, BLOCKS]], base=0, channel_multiplier=0)
            pool.iota(posi[:, :], pattern=[[SEG, NSEG]], base=0, channel_multiplier=EROW)
            pool.iota(node_j[:, :, :], pattern=[[1, P], [0, STEPS]], base=0, channel_multiplier=0,
                      allow_small_or_imprecise_dtypes=True)
            pool.wait_ge(pool_c, 2)
            pool.affine_select(out=identf[:, :], in_=identf[:, :], compare_op=ALU.not_equal, fill=1.0, base=0,
                               pattern=[[-1, P]], channel_multiplier=1)
            pool.affine_select(out=ident[:, 0, :], in_=ident[:, 0, :], compare_op=ALU.not_equal, fill=1.0, base=0,
                               pattern=[[-1, P]], channel_multiplier=1)
            pool.affine_select(out=ident[:, 1, :], in_=ident[:, 1, :], compare_op=ALU.not_equal, fill=-1.0, base=0,
                               pattern=[[-1, P]], channel_multiplier=1).then_inc(pool_c, 1)
            pool.wait_ge(v_rng, 1)
            pool.partition_all_reduce(rangem[:, :], ranges[:, :], P, RMAX).then_inc(pool_rng, 1)
            pool.wait_ge(v_rngi, 1)
            pool.wait_ge(st_t[0], 16 * ((GROUPS + 1) // 2) + 16 * (GROUPS % 2))
            pool.wait_ge(st_t[1], 16 * (GROUPS // 2) + 16 * ((GROUPS + 1) % 2))
            passes = pool.alloc_register("pool_passes")
            pool.reg_mov(passes, 0)

            def gather(b):
                first = pool.value_load(rangei[0:1, bass.ds(b, 1)], min_val=0, max_val=E)
                end = pool.value_load(rangei[0:1, bass.ds(b + BLOCKS, 1)], min_val=0, max_val=E)
                with pool.Fori(first, end, PASS):
                    n = pool.snap(passes)
                    pool.wait_ge(ld_idx, n * 16 + 16)
                    for load in range(LOADS):
                        pool.wait_ge(p_used, n * LOADS + (load + 1))
                        pool.sem_inc(pool_turn, 1)
                        for j in range(load * PER_LOAD, (load + 1) * PER_LOAD):
                            pool.indirect_dma_start(
                                out=rows[:, j, :], out_offset=None, in_=table[:, :],
                                in_offset=bass.IndirectOffsetOnAxis(ap=idx[:, j:j + 1], axis=0)).then_inc(gathered[load], 16)
                    pool.reg_add(passes, passes, 1)

            gather(0)
            pool.wait_ge(v_max, 1)
            pool.partition_all_reduce(wmaxa[:, :], wmax[:, :], P, RMAX).then_inc(pool_max, 1)

            def block(c, q, par, first, second):
                b, last = number(c, q)
                if not last:
                    gather(b + 1)

            main(pool, block)

        @block_ctx.tensor
        def _(pe):
            first_credit(pe, ["p_t1", "p_agg", "p_t2", "p_h", "p_t3", "p_up", "p_dn", "p_t4"])
            pe.sem_inc(p_used, LOADS)
            pe.wait_ge(pool_c, 3)

            for w in range(3):
                with pe.Fori(0, FT) as i:
                    pe.wait_ge(v_cmp, i + (w * FT + 1))
                    done(pe, a_tern, i + w * FT)
                    for g in range(KT):
                        to = tr_ps[:, g * P:(g + 1) * P]
                        pe.matmul(to, above[:, bass.ds(i * KT + g, 1), :].rearrange("p a k -> p (a k)"), ident[:, 0, :],
                                  start=True, stop=False)
                        mm = pe.matmul(to, below[:, bass.ds(i * KT + g, 1), :].rearrange("p a k -> p (a k)"), ident[:, 1, :],
                                       start=False, stop=True)
                    mm.then_inc(p_tern, 1)

            pe.wait_ge(ld_const, 80)
            pe.wait_ge(ld_bias, 64)
            done(pe, a_tern, 3 * FT)
            passes = pe.alloc_register("pe_passes")
            pe.reg_mov(passes, 0)

            def transpose4(source, to=tr_ps):
                for k in range(KT):
                    mm = pe.transpose(to[:, k * P:(k + 1) * P], source(k), identf[:, :])
                return mm

            def step(ffn, s, width=CW):
                c, par = ffn[0], ffn[1]
                kind, i, g, w = place(s)
                to = f_ps[s % 4][:, 0:width]
                if kind == "up":
                    if g >= 2:
                        if g == 2:
                            done(pe, a_up, c * A_UP + (2 * i + w + 1))
                        else:
                            done(pe, v_up, c * V_UP + nth_v_up(i, g - 2, w))
                    elif i:
                        done(pe, v_up, c * V_UP + nth_v_up(i - 1, g + 2, w))
                    else:
                        done(pe, v_dn, c * V_DOWN)
                    lhs, parts = tern[:, w, i * KT + g, :], [x1T[:, par, part, g, 0:width] for part in range(2)]
                    ready = p_up
                else:
                    if g >= 2:
                        if g == 2:
                            done(pe, a_dn, c * A_DOWN + (2 * i + w + 1))
                        else:
                            done(pe, v_dn, c * V_DOWN + nth_v_down(i, g - 2, w))
                    elif i:
                        done(pe, v_dn, c * V_DOWN + nth_v_down(i - 1, FT - 2 + g, w))
                    else:
                        done(pe, v_up, c * V_UP + nth_v_up(FT - 1, g + 2, w))
                    if i == 0:
                        done(pe, v_lo, c * FT + (g + 1))
                    lhs, parts = tern[:, 2, (2 * i + w) * FT + g, :], [hT[:, part, g, 0:width] for part in range(2)]
                    ready = p_dn
                pe.matmul(to, lhs, parts[0], start=True, stop=False)
                pe.matmul(to, lhs, parts[1], start=False, stop=True).then_inc(ready, 1)

            def steps(ffn, a, b, width=CW):
                for s in ffn[2][a:b]:
                    step(ffn, s, width)

            def turn_out(c, t):
                done(pe, v_dn, c * V_DOWN + V_DOWN)
                done(pe, v_out, c * CHUNK + t)
                transpose4(lambda k: yT[:, k, t * P:(t + 1) * P], agg_ps).then_inc(p_t4, 1)

            def turn_x1(b):
                done(pe, a_x1s, b + 1)
                transpose4(lambda k: x1s[:, k * P:(k + 1) * P]).then_inc(p_t3, 1)

            def turned_x1(b):
                done(pe, v_lo1, b + 1)
                done(pe, a_hi1, b + 1)

            def turn_own(b):
                done(pe, a_xs, b + 1)
                transpose4(lambda k: xs[:, k * P:(k + 1) * P]).then_inc(p_t1, 1)

            def sum_load(n, load):
                pe.wait_ge(gathered[load], n * (16 * PER_LOAD) + 16 * PER_LOAD)
                for j in range(load * PER_LOAD, (load + 1) * PER_LOAD):
                    pe.matmul(tr_ps[:, 0:1], hot[:, :, j], ones[:, 0:1], start=False, stop=False, skip_group_check=True)
                    for part in range(2):
                        mm = pe.matmul(agg_ps[:, :], hot[:, :, j], rows[:, j, part * D:(part + 1) * D],
                                       start=False, stop=False, skip_group_check=True)
                mm.then_inc(p_used, 1)

            def block(c, q, par, first, second):
                b, last = number(c, q)
                done(pe, a_ng, b)
                done(pe, a_xsT, b + 1)
                pe.matmul(agg_ps[:, 0:1], zeros[:, :], zeros[:, 0:1], start=True, stop=False, skip_group_check=True)
                pe.matmul(tr_ps[:, 0:1], zeros[:, :], zeros[:, 0:1], start=True, stop=False, skip_group_check=True)
                n = pe.snap(passes)
                done(pe, v_hot, n + 1)
                for load in range(LOADS):
                    sum_load(n, load)
                    steps(first, IN_SUM * load // LOADS, IN_SUM * (load + 1) // LOADS)
                pe.reg_add(passes, passes, 1)
                start = pe.value_load(rangei[0:1, bass.ds(b, 1)], min_val=0, max_val=E)
                end = pe.value_load(rangei[0:1, bass.ds(b + BLOCKS, 1)], min_val=0, max_val=E)
                with pe.If(end > start + PASS):
                    with pe.Fori(start + PASS, end, PASS):
                        n = pe.snap(passes)
                        done(pe, v_hot, n + 1)
                        for load in range(LOADS):
                            sum_load(n, load)
                        pe.reg_add(passes, passes, 1)
                pe.matmul(agg_ps[:, 0:1], zeros[:, :], zeros[:, 0:1], start=False, stop=True, skip_group_check=True)
                pe.matmul(tr_ps[:, 0:1], zeros[:, :], zeros[:, 0:1], start=False, stop=True,
                          skip_group_check=True).then_inc(p_agg, 1)
                done(pe, v_x1, b)
                pe.matmul(h_ps[:, :], onesb[:, :], bparts[:, :], start=True, stop=False)
                behind = not (isinstance(b, int) and b == 0)
                for k in range(KT):
                    if k == KT - 1:
                        done(pe, v_inv, b + 1)
                        if behind:
                            turn_x1(b - 1)
                    pe.matmul(h_ps[:, :], xsT[:, k, :], wself[:, k, :], start=False, stop=False)
                    steps(first, BY_OWN[k], BY_OWN[k + 1])
                if q == 0 and behind:
                    turned_x1(b - 1)
                steps(second, 0, TO_MEAN)
                if q and behind:
                    turned_x1(b - 1)
                done(pe, a_ng, b + 1)
                transpose4(lambda k: ng[:, k * P:(k + 1) * P]).then_inc(p_t2, 1)
                steps(second, TO_MEAN, TO_OWN)
                done(pe, a_ngT, b + 1)
                for k in range(KT):
                    if q == 0 and len(first[2]):
                        turn_out(first[0], k)
                    mm = pe.matmul(h_ps[:, :], ngT[:, k, :], wneigh[:, k, :], start=False, stop=(k == KT - 1))
                    if k == KT - 1:
                        mm.then_inc(p_h, 1)
                    rest = len(second[2]) - TO_OWN
                    steps(second, TO_OWN + rest * k // KT, TO_OWN + rest * (k + 1) // KT)
                    if k == 1 and not last:
                        turn_own(b + 1)
                if q == 0 and len(first[2]):
                    done(pe, v_out, first[0] * CHUNK + CHUNK)

            turn_own(0)
            main(pe, block)
            rest = (FULL - 1, 1, range(QUARTER - LATE, ALL))
            steps(rest, 0, TO_LAST)
            done(pe, a_ngT, BLOCKS)
            turn_x1(BLOCKS - 1)
            turned_x1(BLOCKS - 1)
            steps(rest, TO_LAST, ALL)
            for t in range(CHUNK):
                turn_out(FULL - 1, t)
            steps((FULL, 0, range(ALL)), 0, ALL, P)
            turn_out(FULL, 0)

        @block_ctx.scalar
        def _(act):
            first_credit(act, ["a_norm", "a_high", "a_tern", "a_xs", "a_xx", "a_xsT", "a_ng", "a_ngT", "a_y", "a_x1s",
                               "a_hi1", "a_up", "a_silu", "a_hi", "a_dn"])
            nbank = [agg_ps, h_ps, tr_ps, misc_ps]
            for g in range(GROUPS):
                act.wait_ge(v_stat, g + 1)
                if g >= 2:
                    act.wait_ge(st_t[g % 2], 16 * (g // 2))
                for t in range(GROUP):
                    i = g * GROUP + t
                    done(act, v_low, max(i - 3, 0))
                    act.activation(nbank[i % 4][:, :], xgroup[:, g % 2, t, :], ACT.Identity, bias=nmr_k[:, i:i + 1],
                                   scale=rstd_k[:, i:i + 1]).then_inc(a_norm, 1)
                    done(act, a_norm, i + 1)
                    act.activation(tstage[g % 2][:, t, 0:D], nbank[i % 4][:, :], ACT.Copy).then_inc(a_high, 1)
            for w in range(3):
                with act.Fori(0, FT) as i:
                    done(act, v_low, BLOCKS)
                    act.wait_ge(p_tern, i + (w * FT + 1))
                    act.activation(tern[:, w, bass.ds(i * KT, KT), :].rearrange("p g k -> p (g k)"), tr_ps[:, :],
                                   ACT.Copy).then_inc(a_tern, 1)
            act.wait_ge(ld_const, 80)
            act.wait_ge(v_scl, 1)

            def step(ffn, s, width=CW):
                c = ffn[0]
                kind, i, g, w = place(s)
                if kind == "up" and g == 0:
                    act.wait_ge(p_up, c * UP_STEPS + (s + 2))
                    act.activation(acc[:, w, i % 2, 0:width], f_ps[s % 4][:, 0:width], ACT.Copy,
                                   scale=scl[:, w, i * KT:i * KT + 1]).then_inc(a_up, 1)
                if kind == "up" and g == KT - 1 and w == 1:
                    done(act, v_up, c * V_UP + nth_v_up(i, KT - 1, 0))
                    done(act, v_lo, c * FT + i)
                    act.activation(misc_ps[:, 0:width], acc[:, 0, i % 2, 0:width], ACT.Silu).then_inc(a_silu, 1)
                if kind == "down" and g == 0:
                    act.wait_ge(p_dn, c * DOWN_STEPS + (s - UP_STEPS + 2))
                    if i == 0:
                        done(act, p_t4, c * CHUNK)
                    d = 2 * i + w
                    act.activation(yT[:, d, 0:width], f_ps[s % 4][:, 0:width], ACT.Copy,
                                   scale=scl[:, 2, d * FT:d * FT + 1]).then_inc(a_dn, 1)
                if s % (2 * KT) == 4 and 0 < s <= UP_STEPS + 4:
                    f = s // (2 * KT) - 1
                    if f >= 0:
                        done(act, v_h, c * FT + (f + 1))
                        act.activation(hT[:, 0, f, 0:width], misc_ps[:, 0:width], ACT.Copy).then_inc(a_hi, 1)

            def steps(ffn, a, b, width=CW):
                for s in ffn[2][a:b]:
                    step(ffn, s, width)

            def slope(b):
                done(act, v_t2, b + 1)
                act.activation(neg[:, :], t2[:, :], ACT.Relu, scale=-1.0)
                act.activation(h_ps[:, :], t2[:, :], ACT.Relu).then_inc(a_y, 1)

            def norm_x1(b, q, par):
                done(act, v_n1, b + 1)
                done(act, p_t3, b)
                act.activation(x1s[:, :], x1[:, par, q, :], ACT.Identity, bias=small[:, 13:14],
                               scale=small[:, 10:11]).then_inc(a_x1s, 1)

            def high_x1(b, q, par):
                done(act, p_t3, b + 1)
                act.activation(x1T[:, par, 0, :, q * P:(q + 1) * P], tr_ps[:, :].rearrange("p (k n) -> p k n", k=KT),
                               ACT.Copy, scale=XSCALE).then_inc(a_hi1, 1)

            def own_rows(b, q):
                act.wait_ge(ld_x[q % 2], (b // 2 + 1) * 16 if isinstance(b, int) else (b - q % 2) * 8 + 16)
                done(act, p_t1, b)
                act.activation(xs[:, :], xin[:, q % 2, :], ACT.Identity, bias=nmr[:, bass.ds(b, 1)],
                               scale=rstd[:, bass.ds(b, 1)]).then_inc(a_xs, 1)
                done(act, v_x1, max(b - 1, 0) if isinstance(b, int) else b - 1)
                act.activation(xx[:, q % 2, :], xin[:, q % 2, :], ACT.Identity, bias=nmr[:, bass.ds(b, 1)],
                               scale=one_r[:, bass.ds(b, 1)]).then_inc(a_xx, 1)

            def own_turned(b):
                done(act, p_t1, b + 1)
                done(act, p_t2, b)
                act.activation(xsT[:, :, :].rearrange("p k n -> p (k n)"), tr_ps[:, :], ACT.Copy).then_inc(a_xsT, 1)

            def block(c, q, par, first, second):
                b, last = number(c, q)
                behind = not (isinstance(b, int) and b == 0)
                at = ((q - 1) % CHUNK, par if q else 1 - par)
                steps(first, 0, TO_SLOPE)
                if behind:
                    slope(b - 1)
                steps(first, TO_SLOPE, IN_SUM)
                if behind:
                    norm_x1(b - 1, *at)
                done(act, p_agg, b + 1)
                done(act, v_inv, b + 1)
                done(act, p_t2, b)
                act.activation(ng[:, :], agg_ps[:, :], ACT.Copy, scale=small[:, 1:2]).then_inc(a_ng, 1)
                steps(first, IN_SUM, LATE)
                if behind:
                    high_x1(b - 1, *at)
                steps(second, 0, TO_MEAN)
                done(act, p_t2, b + 1)
                act.activation(ngT[:, :, :].rearrange("p k n -> p (k n)"), tr_ps[:, :], ACT.Copy).then_inc(a_ngT, 1)
                steps(second, TO_MEAN, TO_OWN)
                if not last:
                    own_rows(b + 1, q + 1)
                half = TO_OWN + (QUARTER - LATE - TO_OWN) // 2
                steps(second, TO_OWN, half)
                if not last:
                    own_turned(b + 1)
                steps(second, half, QUARTER)

            own_rows(0, 0)
            own_turned(0)
            main(act, block)
            rest = (FULL - 1, 1, range(QUARTER - LATE, ALL))
            steps(rest, 0, TO_SLOPE)
            slope(BLOCKS - 1)
            steps(rest, TO_SLOPE, LATE)
            norm_x1(BLOCKS - 1, 0, 0)
            steps(rest, LATE, TO_LAST)
            high_x1(BLOCKS - 1, 0, 0)
            steps(rest, TO_LAST, ALL)
            steps((FULL, 0, range(ALL)), 0, ALL, P)

        @block_ctx.vector
        def _(dve):
            first_credit(dve, ["v_low", "v_dl", "v_hot", "v_deg", "v_inv", "v_t2", "v_x1", "v_n1", "v_lo1", "v_up", "v_h",
                               "v_lo", "v_dn", "v_out"])

            class Chain:

                def __init__(self, s, start=0):
                    self.s, self.n, self.start = s, 0, start

                def step(self, ins, fill=None):
                    ins.then_inc(self.s, 1)
                    self.n += 1
                    if fill is not None:
                        fill()
                    dve.wait_ge(self.s, self.start + self.n)

            def rsqrt(chain, v, y, a, vh, yc, fill=None):
                chain.step(dve.tensor_scalar(a, v, EPS, None, ALU.add))
                dve.tensor_scalar(vh, a, 64.0 / 9.0, None, ALU.mult)
                chain.step(dve.tensor_scalar(y.bitcast(I32), a.bitcast(I32), -0.5, RSQRT_GUESS, ALU.mult, ALU.add))
                if y.shape[-1] == 1:
                    dve.tensor_scalar(yc, y, RSQRT_GAIN * 3.0 / 8.0, None, ALU.mult)
                    chain.step(dve.tensor_scalar(a, y, y, a, ALU.mult, ALU.mult), fill)
                else:
                    dve.tensor_scalar(yc, y, RSQRT_GAIN * 3.0 / 8.0, None, ALU.mult)
                    chain.step(dve.tensor_tensor(y, y, y, ALU.mult))
                    chain.step(dve.tensor_tensor(a, a, y, ALU.mult))
                chain.step(dve.scalar_tensor_tensor(out=yc, in0=a, scalar=RSQRT_FIRST, in1=yc, op0=ALU.subtract,
                                                    op1=ALU.mult), fill)
                if y.shape[-1] == 1:
                    chain.step(dve.tensor_scalar(a, yc, yc, vh, ALU.mult, ALU.mult))
                else:
                    chain.step(dve.tensor_tensor(a, yc, yc, ALU.mult))
                    chain.step(dve.tensor_tensor(a, a, vh, ALU.mult))
                chain.step(dve.scalar_tensor_tensor(out=a, in0=a, scalar=10.0 / 3.0, in1=a, op0=ALU.subtract, op1=ALU.mult))
                chain.step(dve.scalar_tensor_tensor(out=y, in0=a, scalar=5.0, in1=yc, op0=ALU.add, op1=ALU.mult), fill)

            pro = Chain(v_pro)
            dve.wait_ge(ld_dst, 16)
            pro.step(dve.tensor_copy(dst_f, dst_i))
            dve.sem_inc(v_dst, 1)
            seg3 = dst_f.rearrange("p (s e) -> p s e", e=SEG)
            dve.tensor_reduce(segs[0:EP, 0, :], seg3, AX.X, ALU.min)
            dve.tensor_reduce(segs[0:EP, 1, :], seg3, AX.X, ALU.max)
            dve.wait_ge(pool_c, 3)
            dve.tensor_copy(base[:, :], rangei[:, 0:BLOCKS])
            pro.step(dve.tensor_scalar(top[:, :], rangei[:, 0:BLOCKS], float(P - 1), None, ALU.add))
            dve.tensor_scalar(segs[:, 2, :], posi[:, :], -1.0, BIG, ALU.mult, ALU.add)
            pro.step(dve.tensor_scalar(segs[:, 3, :], posi[:, :], float(SEG), None, ALU.add))

            def over_blocks(v):
                return v[0:EP, None, :].broadcast_to((EP, BLOCKS, NSEG))

            def over_segs(v):
                return v[0:EP, :, None].broadcast_to((EP, BLOCKS, NSEG))

            dve.tensor_tensor(hit[0], over_blocks(segs[:, 0, :]), over_segs(top[:, :]), ALU.is_le)
            pro.step(dve.tensor_tensor(hit[1], over_blocks(segs[:, 1, :]), over_segs(base[:, :]), ALU.is_ge))
            pro.step(dve.tensor_tensor(hit[0], hit[0], hit[1], ALU.mult))
            dve.tensor_tensor(hit[1], hit[0], over_blocks(segs[:, 2, :]), ALU.mult)
            pro.step(dve.tensor_tensor(hit[2], hit[0], over_blocks(segs[:, 3, :]), ALU.mult))
            dve.tensor_reduce(ranges[0:EP, 0:BLOCKS], hit[1], AX.X, ALU.max)
            dve.tensor_reduce(ranges[0:EP, BLOCKS:2 * BLOCKS], hit[2], AX.X, ALU.max).then_inc(v_rng, 1)
            dve.wait_ge(ld_bias, 16)
            for i in range(3):
                pro.step(dve.tensor_copy(browb[:, i, :], brow[:, i, :]))
                if i < 2:
                    pro.step(dve.tensor_tensor(brow[:, i + 1, :], brow[:, i, :], browb[:, i, :], ALU.subtract))
            dve.sem_inc(v_bias, 1)
            dve.wait_ge(pool_rng, 1)
            pro.step(dve.tensor_scalar(rangem[:, 0:BLOCKS], rangem[:, 0:BLOCKS], -1.0, BIG, ALU.mult, ALU.add))
            pro.step(dve.tensor_scalar(rangem[:, 0:BLOCKS], rangem[:, 0:BLOCKS], float(E), None, ALU.min))
            dve.tensor_copy(rangei[:, :], rangem[:, :]).then_inc(v_rngi, 1)

            loaded = [0, 0]
            nbank = [agg_ps, h_ps, tr_ps, misc_ps]

            def group_stats(g):
                loaded[g % 2] += 32 if g == GROUPS - 1 else 16
                dve.wait_ge(ld_xg[g % 2], loaded[g % 2])
                lo, hi = g * GROUP, (g + 1) * GROUP
                for t in range(GROUP):
                    ins = dve.bn_stats(stats6[:, t, :], xgroup[:, g % 2, t, :])
                pro.step(ins)
                for t in range(GROUP):
                    ins = dve.bn_aggr(mv[:, lo + t, :], stats6[:, t, :])
                pro.step(ins)
                rsqrt(pro, mv[:, lo:hi, 1], rstd[:, lo:hi], tmp[:, 0, :], tmp[:, 1, :], tmp[:, 2, :])
                dve.tensor_scalar(rstd_k[:, lo:hi], rstd[:, lo:hi], XSCALE, None, ALU.mult)
                dve.tensor_scalar(one_r[:, lo:hi], rstd[:, lo:hi], 1.0, None, ALU.add)
                pro.step(dve.scalar_tensor_tensor(out=nmr[:, lo:hi], in0=mv[:, lo:hi, 0], scalar=-1.0,
                                                  in1=rstd[:, lo:hi], op0=ALU.mult, op1=ALU.mult))
                dve.tensor_scalar(nmr_k[:, lo:hi], nmr[:, lo:hi], XSCALE, None, ALU.mult).then_inc(v_stat, 1)

            def group_low(g):
                for t in range(GROUP):
                    i = g * GROUP + t
                    done(dve, a_high, i + 1)
                    dve.tensor_tensor(tstage[g % 2][:, t, D:2 * D], nbank[i % 4][:, :], tstage[g % 2][:, t, 0:D],
                                      ALU.subtract).then_inc(v_low, 1)

            group_stats(0)
            for g in range(GROUPS):
                if g + 1 < GROUPS:
                    group_stats(g + 1)
                group_low(g)

            passes = dve.alloc_register("dve_passes")
            dve.reg_mov(passes, 0)

            def one_hot_pass(b):
                n = dve.snap(passes)
                dve.wait_ge(ld_dv, n * 16 + 16)
                done(dve, v_hot, n)
                dve.tensor_scalar(dstl[:, :], dstv[:, :], base[:, bass.ds(b, 1)], None, ALU.subtract).then_inc(v_dl, 1)
                done(dve, v_dl, n + 1)
                dve.wait_ge(p_used, n * LOADS + LOADS)
                dve.tensor_tensor(hot[:, :, :], dstl[:, None, :].broadcast_to((P, P, STEPS)), node_j[:, :, :],
                                  ALU.is_equal).then_inc(v_hot, 1)
                dve.reg_add(passes, passes, 1)

            def one_hot_more(b):
                start = dve.value_load(rangei[0:1, bass.ds(b, 1)], min_val=0, max_val=E)
                end = dve.value_load(rangei[0:1, bass.ds(b + BLOCKS, 1)], min_val=0, max_val=E)
                with dve.If(end > start + PASS):
                    with dve.Fori(start + PASS, end, PASS):
                        one_hot_pass(b)

            one_hot_pass(0)

            for w in range(3):
                dve.wait_ge(ld_w[w], 16)
                pro.step(dve.tensor_reduce(scl[:, w, :], wstage, AX.X, ALU.add, apply_absolute_value=True))
                pro.step(dve.tensor_scalar(scl[:, w, :], scl[:, w, :], 1.0 / P, EPS, ALU.mult, ALU.add))
                dve.tensor_scalar(half[:, 0, :], scl[:, w, :], 0.5, None, ALU.mult)
                pro.step(dve.tensor_scalar(half[:, 1, :], scl[:, w, :], -0.5, None, ALU.mult))
                if w == 0:
                    dve.wait_ge(st_t[0], 16 * ((GROUPS + 1) // 2) + 16 * (GROUPS % 2))
                    dve.wait_ge(st_t[1], 16 * (GROUPS // 2) + 16 * ((GROUPS + 1) % 2))
                else:
                    dve.wait_ge(p_tern, w * FT)
                with dve.Fori(0, FT) as i:
                    for g in range(KT):
                        j = bass.ds(i * KT + g, 1)
                        dve.tensor_scalar(above[:, j, :], wstage[:, j, :], half[:, 0, j], None, ALU.is_gt)
                        ins = dve.tensor_scalar(below[:, j, :], wstage[:, j, :], half[:, 1, j], None, ALU.is_lt)
                    ins.then_inc(v_cmp, 1)
            dve.tensor_reduce(wmax[:, 0:1], scl[:, 0, :], AX.X, ALU.max)
            dve.tensor_reduce(wmax[:, 1:2], scl[:, 1, :], AX.X, ALU.max).then_inc(v_max, 1)
            dve.wait_ge(pool_max, 1)
            pro.step(dve.tensor_scalar(hsc[:, 0:1], wmaxa[:, 0:1], wmaxa[:, 1:2], float(D * D) / 2.0 ** 15, ALU.mult, ALU.mult))
            pro.step(dve.reciprocal(hsc[:, 1:2], hsc[:, 0:1]))
            pro.step(dve.tensor_scalar(hsc[:, 2:3].bitcast(I32), hsc[:, 1:2].bitcast(I32), EXPONENT_BITS, None, ALU.bitwise_and))
            pro.step(dve.tensor_scalar(hsc[:, 3:4].bitcast(I32), hsc[:, 2:3].bitcast(I32), -1.0, TWICE_BIAS_BITS, ALU.mult, ALU.add))
            dve.tensor_scalar(scl[:, 0, :], scl[:, 0, :], 1.0 / XSCALE, None, ALU.mult)
            dve.tensor_scalar(scl[:, 1, :], scl[:, 1, :], hsc[:, 2:3], 1.0 / XSCALE, ALU.mult, ALU.mult)
            pro.step(dve.tensor_scalar(scl[:, 2, :], scl[:, 2, :], hsc[:, 3:4], None, ALU.mult))
            dve.sem_inc(v_scl, 1)
            dve.wait_ge(ld_const, 80)
            pro.step(dve.tensor_scalar(neg_alpha[:, :], alpha_c[:, :], -1.0, None, ALU.mult))

            def step(ffn, s, width=CW):
                c = ffn[0]
                kind, i, g, w = place(s)
                ps = f_ps[s % 4][:, 0:width]
                if kind == "up" and g:
                    dve.wait_ge(p_up, c * UP_STEPS + (s + 2))
                    if g == 1:
                        done(dve, a_up, c * A_UP + (2 * i + w + 1))
                    else:
                        done(dve, v_up, c * V_UP + nth_v_up(i, g - 1, w))
                    a = acc[:, w, i % 2, 0:width]
                    dve.scalar_tensor_tensor(out=a, in0=ps, scalar=scl[:, w, i * KT + g:i * KT + g + 1], in1=a,
                                             op0=ALU.mult, op1=ALU.add).then_inc(v_up, 1)
                if kind == "down" and g:
                    d = 2 * i + w
                    dve.wait_ge(p_dn, c * DOWN_STEPS + (s - UP_STEPS + 2))
                    if g == 1:
                        done(dve, a_dn, c * A_DOWN + (d + 1))
                    else:
                        done(dve, v_dn, c * V_DOWN + nth_v_down(i, g - 1, w))
                    y = yT[:, d, 0:width]
                    dve.scalar_tensor_tensor(out=y, in0=ps, scalar=scl[:, 2, d * FT + g:d * FT + g + 1], in1=y,
                                             op0=ALU.mult, op1=ALU.add).then_inc(v_dn, 1)
                f = s // (2 * KT) - 1
                if 0 <= f < FT and s % (2 * KT) == 3:
                    done(dve, a_silu, c * FT + (f + 1))
                    done(dve, v_up, c * V_UP + nth_v_up(f, KT - 1, 1))
                    dve.tensor_tensor(misc_ps[:, 0:width], misc_ps[:, 0:width], acc[:, 1, f % 2, 0:width],
                                      ALU.mult).then_inc(v_h, 1)
                if 0 <= f < FT and s % (2 * KT) == 6:
                    done(dve, a_hi, c * FT + (f + 1))
                    dve.tensor_tensor(hT[:, 1, f, 0:width], misc_ps[:, 0:width], hT[:, 0, f, 0:width],
                                      ALU.subtract).then_inc(v_lo, 1)

            def steps(ffn, a, b, width=CW):
                for s in ffn[2][a:b]:
                    step(ffn, s, width)

            def norms(b, q, par, ffn):
                chain = Chain(v_chain, b * CHAIN_STEPS)
                todo = iter(ffn[2][0:IN_SUM])
                used = [0]

                def fill():
                    for s in todo:
                        step(ffn, s)
                        used[0] += 1
                        return

                done(dve, p_h, b + 1)
                chain.step(dve.bn_stats(st6[:, :], h_ps[:, :]), fill)
                dve.sem_inc(dve_turn, 1)
                chain.step(dve.bn_aggr(small[:, 2:4], st6[:, :]), fill)
                rsqrt(chain, small[:, 3:4], small[:, 4:5], small[:, 5:6], small[:, 6:7], small[:, 7:8], fill)
                chain.step(dve.scalar_tensor_tensor(out=h_ps[:, :], in0=h_ps[:, :], scalar=small[:, 2:3],
                                                    in1=gamma_b[:, :], op0=ALU.subtract, op1=ALU.mult), fill)
                assert used[0] in (0, TO_SLOPE - 1)
                done(dve, a_y, b)
                dve.scalar_tensor_tensor(out=t2[:, :], in0=h_ps[:, :], scalar=small[:, 4:5], in1=beta_b[:, :],
                                         op0=ALU.mult, op1=ALU.add).then_inc(v_t2, 1)
                fill()
                done(dve, a_y, b + 1)
                done(dve, a_xx, b + 1)
                chain.step(dve.scalar_tensor_tensor(out=xx[:, q % 2, :], in0=neg[:, :], scalar=neg_alpha[:, 0:1],
                                                    in1=xx[:, q % 2, :], op0=ALU.mult, op1=ALU.add), fill)
                dve.tensor_tensor(x1[:, par, q, :], h_ps[:, :], xx[:, q % 2, :], ALU.add).then_inc(v_x1, 1)
                done(dve, v_x1, b + 1)
                chain.step(dve.bn_stats(st6[:, :], x1[:, par, q, :]), fill)
                done(dve, a_x1s, b)
                dve.sem_inc(dve_turn, 1)
                chain.step(dve.bn_aggr(small[:, 8:10], st6[:, :]), fill)
                rsqrt(chain, small[:, 9:10], small[:, 10:11], small[:, 11:12], small[:, 12:13], small[:, 14:15], fill)
                dve.tensor_scalar(small[:, 13:14], small[:, 8:9], small[:, 10:11], -1.0, ALU.mult,
                                  ALU.mult).then_inc(v_n1, 1)
                assert chain.n == CHAIN_STEPS, chain.n
                for s in todo:
                    step(ffn, s)

            def low_x1(b, q, par):
                done(dve, p_t3, b + 1)
                done(dve, a_hi1, b + 1)
                dve.scalar_tensor_tensor(out=x1T[:, par, 1, :, q * P:(q + 1) * P],
                                         in0=tr_ps[:, :].rearrange("p (k n) -> p k n", k=KT), scalar=XSCALE,
                                         in1=x1T[:, par, 0, :, q * P:(q + 1) * P], op0=ALU.mult,
                                         op1=ALU.subtract).then_inc(v_lo1, 1)

            def add_out(c, par, t):
                done(dve, p_t4, c * CHUNK + (t + 1))
                done(dve, stored, c * CHUNK + max(t - 1, 0))
                dve.tensor_tensor(outb[:, t % 2, :], agg_ps[:, :], x1[:, par, t, :], ALU.add).then_inc(v_out, 1)

            def block(c, q, par, first, second):
                b, last = number(c, q)
                behind = not (isinstance(b, int) and b == 0)
                at = ((q - 1) % CHUNK, par if q else 1 - par)
                if behind:
                    norms(b - 1, *at, first)
                one_hot_more(b)
                done(dve, p_agg, b + 1)
                done(dve, a_ng, b)
                dve.tensor_scalar(small[:, 0:1], tr_ps[:, 0:1], 1.0, XSCALE, ALU.max, ALU.mult).then_inc(v_deg, 1)
                done(dve, v_deg, b + 1)
                dve.reciprocal(small[:, 1:2], small[:, 0:1]).then_inc(v_inv, 1)
                steps(first, IN_SUM, LATE)
                if behind:
                    low_x1(b - 1, *at)
                steps(second, 0, TO_MEAN)
                if not last:
                    one_hot_pass(b + 1)
                steps(second, TO_MEAN, TO_OWN)
                rest = len(second[2]) - TO_OWN
                for k in range(KT):
                    if q == 0 and len(first[2]):
                        add_out(first[0], first[1], k)
                    if rest > 0:
                        steps(second, TO_OWN + rest * k // KT, TO_OWN + rest * (k + 1) // KT)

            main(dve, block)
            rest = (FULL - 1, 1, range(QUARTER - LATE, ALL))
            norms(BLOCKS - 1, 0, 0, rest)
            steps(rest, IN_SUM, TO_LAST)
            low_x1(BLOCKS - 1, 0, 0)
            steps(rest, TO_LAST, ALL)
            for t in range(CHUNK):
                add_out(FULL - 1, 1, t)
            steps((FULL, 0, range(ALL)), 0, ALL, P)
            add_out(FULL, 0, 0)


CHAIN_STEPS = 2 * (2 + 7) + 2

_INS = ["x", "src", "dst", "L0_gnn_W_self", "L0_gnn_b_self", "L0_gnn_W_neigh", "L0_gnn_gamma", "L0_gnn_beta",
        "L0_gnn_alpha", "L0_ffn_w_gate", "L0_ffn_w_up", "L0_ffn_w_down"]


def kernel(**inputs):
    import concourse.bacc as bacc
    from concourse.bass_utils import run_bass_kernel_spmd

    nc = bacc.Bacc("TRN2", target_bir_lowering=False, num_devices=1)
    arrays, args = {}, []
    for name in _INS:
        a = np.ascontiguousarray(inputs[name])
        if a.ndim == 0:
            a = a.reshape(1)
        arrays[f"in_{name}"] = a
        args.append(nc.dram_tensor(f"in_{name}", a.shape, mybir.dt.from_np(a.dtype), kind="ExternalInput").ap())
    shape = np.shape(inputs["x"])
    args.append(nc.dram_tensor("out_nodes", shape, F32, kind="ExternalOutput").ap())
    build(nc, *args)
    r = run_bass_kernel_spmd(nc, [arrays], core_ids=[0])
    return r.results[0]["out_nodes"]
```

```python
from contextlib import ExitStack

import numpy as np

import concourse.bass as bass
from concourse import mybir

ALU = mybir.AluOpType
ACT = mybir.ActivationFunctionType
F32 = mybir.dt.float32
F16 = mybir.dt.float16
BF16 = mybir.dt.bfloat16
I32 = mybir.dt.int32
AX = mybir.AxisListType
RMAX = bass.bass_isa.ReduceOp.max

P = 128
EPS = 1e-5
XSCALE = 1024.0
RSQRT_GUESS = float(0x5F1FFFF9 - (1 << 31))
RSQRT_FIRST, RSQRT_GAIN = 2.38924456, 0.703952253
EXPONENT_BITS = 0x7F800000
TWICE_BIAS_BITS = float(0x7F000000)
STEPS = 18
PER_LOAD = 3
LOADS = STEPS // PER_LOAD
BIG = float(1 << 17)


def build(nc, x, src, dst, W_self, b_self, W_neigh, gamma, beta, alpha, w_gate, w_up, w_down, out):
    N, D = x.shape
    E = src.shape[0]
    FFN = w_gate.shape[0]
    KT = D // P
    FT = FFN // P
    NG = FT * KT
    BLOCKS = -(-N // P)
    LAST = N - (BLOCKS - 1) * P
    CHUNK = 4
    CW = CHUNK * P
    FULL = (BLOCKS - 1) // CHUNK
    assert BLOCKS == FULL * CHUNK + 1 and FULL % 2 == 0 and D == CW
    PASS = STEPS * P
    EP = 125
    SEG = 17
    EROW = E // EP
    NSEG = EROW // SEG
    assert EP * NSEG * SEG == E
    GROUP = 7
    GROUPS = BLOCKS // GROUP
    assert GROUP * GROUPS == BLOCKS

    table = nc.dram_tensor("node_table", (N, 2 * D), F16, kind="Internal").ap()
    src_pad = nc.dram_tensor("src_pad", (E + PASS,), I32, kind="Internal").ap()
    dst_pad = nc.dram_tensor("dst_pad", (E + PASS,), F32, kind="Internal").ap()

    with ExitStack() as ctx:
        def sb(name, shape, dt):
            return ctx.enter_context(nc.sbuf_tensor(name, shape, dt))

        def bank(name):
            return ctx.enter_context(nc.psum_tensor(name, [P, 512], F32))

        sems = {}

        def sem(name):
            sems[name] = ctx.enter_context(nc.semaphore(name))
            return sems[name]

        rows = sb("rows", [P, STEPS, 2 * D], F16)
        wself = sb("wself", [P, KT, D], F32)
        wneigh = sb("wneigh", [P, KT, D], F32)
        tern = sb("tern", [P, 3, NG, P], F16)
        x1 = sb("x1", [P, 2, CHUNK, D], F32)
        x1T = sb("x1T", [P, 2, 2, KT, CW], F16)
        hT = sb("hT", [P, 2, FT, CW], F16)
        yT = sb("yT", [P, KT, CW], F32)
        acc = sb("acc", [P, 2, 2, CW], F32)
        xin = sb("xin", [P, 2, D], F32)
        xs = sb("xs", [P, D], F32)
        xx = sb("xx", [P, 2, D], F32)
        neg = sb("neg", [P, D], F32)
        t2 = sb("t2", [P, D], F32)
        x1s = sb("x1s", [P, D], F32)
        outb = sb("outb", [P, 2, D], F32)
        xsT = sb("xsT", [P, KT, P], F32)
        ng = sb("ng", [P, D], F32)
        ngT = sb("ngT", [P, KT, P], F32)
        gamma_b = sb("gamma_b", [P, D], F32)
        beta_b = sb("beta_b", [P, D], F32)
        hot = sb("hot", [P, P, STEPS], F16)
        node_j = sb("node_j", [P, P, STEPS], F16)
        idx = sb("idx", [P, STEPS], I32)
        dstv = sb("dstv", [P, STEPS], F32)
        dstl = sb("dstl", [P, STEPS], F16)
        identf = sb("identf", [P, P], F32)
        ident = sb("ident", [P, 2, P], F16)
        zeros = sb("zeros", [P, P], F16)
        ones = sb("ones", [P, P], F16)
        bparts = sb("bparts", [3, D], BF16)
        onesb = sb("onesb", [3, P], BF16)
        alpha_c = sb("alpha_c", [P, 1], F32)
        neg_alpha = sb("neg_alpha", [P, 1], F32)
        base = sb("base", [P, BLOCKS], F32)
        top = sb("top", [P, BLOCKS], F32)
        stats6 = sb("stats6", [P, GROUP, 6], F32)
        mv = sb("mv", [P, BLOCKS, 2], F32)
        rstd = sb("rstd", [P, BLOCKS], F32)
        nmr = sb("nmr", [P, BLOCKS], F32)
        rstd_k = sb("rstd_k", [P, BLOCKS], F32)
        nmr_k = sb("nmr_k", [P, BLOCKS], F32)
        one_r = sb("one_r", [P, BLOCKS], F32)
        tmp = sb("tmp", [P, 4, GROUP], F32)
        small = sb("small", [P, 32], F32)
        st6 = sb("st6", [P, 6], F32)
        segs = sb("segs", [P, 4, NSEG], F32)
        posi = sb("posi", [P, NSEG], I32)
        ranges = sb("ranges", [P, 2 * BLOCKS], F32)
        rangem = sb("rangem", [P, 2 * BLOCKS], F32)
        rangei = sb("rangei", [P, 3 * BLOCKS], I32)
        padi = sb("padi", [P, STEPS], I32)
        padf = sb("padf", [P, STEPS], F32)
        scl = sb("scl", [P, 3, NG], F32)
        half = sb("half", [P, 2, NG], F32)
        wmax = sb("wmax", [P, 2], F32)
        wmaxa = sb("wmaxa", [P, 2], F32)
        hsc = sb("hsc", [P, 4], F32)

        agg_ps = bank("agg_ps")
        h_ps = bank("h_ps")
        tr_ps = bank("tr_ps")
        misc_ps = bank("misc_ps")
        f_ps = [bank(f"f_ps{i}") for i in range(4)]

        xgroup = [half_ring[:, g * GROUP * D:(g + 1) * GROUP * D].rearrange("p (t d) -> p t d", t=GROUP)
                  for half_ring in (rows[:, :, :].rearrange("p a b -> p (a b)").bitcast(F32),
                                    tern[:, :, :, :].rearrange("p w g k -> p (w g k)").bitcast(F32)) for g in range(2)]
        RING = len(xgroup)
        tstage = [x1[:, :, :, :].rearrange("p a b c -> p (a b c)").bitcast(F16)[:, 0:GROUP * 2 * D].rearrange(
            "p (t d) -> p t d", t=GROUP),
            x1T[:, :, :, :, :].rearrange("p a b c d -> p (a b c d)")[:, 0:GROUP * 2 * D].rearrange(
            "p (t d) -> p t d", t=GROUP)]
        wstage = hT[:, :, :, :].rearrange("p a b c -> p (a b c)").bitcast(F32).rearrange(
            "p (g k) -> p g k", g=NG)
        WRING = 4
        wcmp = x1T[:, 1, :, :, :].rearrange("p b c d -> p (b c d)").rearrange(
            "p (r s g k) -> p r s g k", r=WRING, s=2, g=KT)
        tern32 = tern[:, :, :, :].rearrange("p w g k -> p w (g k)").bitcast(F32)
        hit = [tern32[0:EP, w, 0:BLOCKS * NSEG].rearrange("p (b s) -> p b s", b=BLOCKS) for w in range(3)]
        yflat = yT[:, :, :].rearrange("p a b -> p (a b)")
        dst_i = yflat[0:EP, 0:EROW].bitcast(I32)
        dst_f = yflat[0:EP, EROW:2 * EROW]

        brow = acc[0:1, :, :, :].rearrange("p a b c -> p (a b) c")
        browb = outb[0:1, :, :].rearrange("p a b -> p (a b)").bitcast(BF16)[:, 0:3 * D].rearrange("p (i d) -> p i d", i=3)

        nbank = [agg_ps, h_ps, tr_ps, misc_ps] + f_ps

        ld_dst, ld_const, ld_bias, ld_pads = sem("ld_dst"), sem("ld_const"), sem("ld_bias"), sem("ld_pads")
        ld_w = [sem(f"ld_w{w}") for w in range(3)]
        ld_xg = [sem(f"ld_xg{i}") for i in range(RING)]
        st_t = [sem(f"st_t{i}") for i in range(2)]
        ld_x = [sem(f"ld_x{i}") for i in range(2)]
        ld_idx, ld_dv = sem("ld_idx"), sem("ld_dv")
        gathered = [sem(f"gathered{i}") for i in range(LOADS)]
        st_out = sem("st_out")
        pool_c, pool_rng, pool_max = sem("pool_c"), sem("pool_rng"), sem("pool_max")
        v_pro, v_dst, v_rng, v_rngi, v_bias = sem("v_pro"), sem("v_dst"), sem("v_rng"), sem("v_rngi"), sem("v_bias")
        v_stat, v_low, v_cmp, v_max, v_scl = sem("v_stat"), sem("v_low"), sem("v_cmp"), sem("v_max"), sem("v_scl")
        a_norm, a_high, p_tern, a_tern = sem("a_norm"), sem("a_high"), sem("p_tern"), sem("a_tern")
        v_dl, p_used, v_hot, p_agg, v_deg, v_inv = (sem(n) for n in ("v_dl", "p_used", "v_hot", "p_agg", "v_deg", "v_inv"))
        a_xs, a_xx, p_t1, a_xsT, a_ng, p_t2, a_ngT, p_h = (
            sem(n) for n in ("a_xs", "a_xx", "p_t1", "a_xsT", "a_ng", "p_t2", "a_ngT", "p_h"))
        v_chain, v_t2, a_y, v_x1, v_n1, a_x1s, p_t3, a_hi1, v_lo1 = (
            sem(n) for n in ("v_chain", "v_t2", "a_y", "v_x1", "v_n1", "a_x1s", "p_t3", "a_hi1", "v_lo1"))
        p_up, p_dn, p_t4, a_up, a_dn, v_up, v_dn = (
            sem(n) for n in ("p_up", "p_dn", "p_t4", "a_up", "a_dn", "v_up", "v_dn"))
        a_silu, v_h, a_hi, v_lo, v_out, stored = (
            sem(n) for n in ("a_silu", "v_h", "a_hi", "v_lo", "v_out", "stored"))
        sp_turn, pool_turn, dve_turn = sem("sp_turn"), sem("pool_turn"), sem("dve_turn")

        def done(eng, s, n):
            eng.wait_ge(s, n + 1)

        def first_credit(eng, names):
            for name in names:
                eng.sem_inc(sems[name], 1)

        UP_STEPS = FT * KT * 2
        DOWN_STEPS = KT * FT
        ALL = UP_STEPS + DOWN_STEPS
        QUARTER = ALL // CHUNK
        LATE = 18
        IN_SUM = 14
        BY_OWN = (IN_SUM, IN_SUM, IN_SUM + 1, IN_SUM + 2, LATE)
        assert ALL % CHUNK == 0 and UP_STEPS % 4 == 0

        def place(s):
            if s < UP_STEPS:
                return ("up", s // (2 * KT), s // 2 % KT, s % 2)
            s -= UP_STEPS
            return ("down", s // (2 * FT), s // 2 % FT, s % 2)

        V_UP, V_DOWN, A_UP, A_DOWN = 2 * (KT - 1) * FT, (FT - 1) * KT, 2 * FT, KT

        def nth_v_up(f, g, w):
            return f * 2 * (KT - 1) + (g - 1) * 2 + w + 1

        def nth_v_down(pair, g, e):
            return pair * 2 * (FT - 1) + (g - 1) * 2 + e + 1

        def more_passes(eng, b, one_pass):
            beyond = eng.value_load(rangei[0:1, bass.ds(b + 2 * BLOCKS, 1)], min_val=0, max_val=E)
            with eng.If(beyond > 0):
                with eng.Fori(0, beyond, PASS):
                    one_pass()

        NONE = (0, 0, range(0))

        def beside(c, q, par):
            at = QUARTER * ((q - 1) % CHUNK)
            late = range(at + QUARTER - LATE, at + QUARTER)
            first = (c - 2, par, late) if q == 0 else (c - 1, 1 - par, late)
            second = (c - 1, 1 - par, range(QUARTER * q, QUARTER * (q + 1) - LATE))
            return first, second

        def main(eng, block):
            for q in range(CHUNK):
                block(0, q, 0, NONE, NONE)
            for q in range(CHUNK):
                first, second = beside(1, q, 1)
                block(1, q, 1, first if q else NONE, second)
            with eng.Fori(0, (FULL - 4) // 2) as u:
                for h in range(2):
                    for q in range(CHUNK):
                        block(u * 2 + (2 + h), q, h, *beside(u * 2 + (2 + h), q, h))
            for c in range(FULL - 2, FULL):
                for q in range(CHUNK):
                    block(c, q, c % 2, *beside(c, q, c % 2))
            block(FULL, 0, 0, *beside(FULL, 0, 0))

        def number(c, q):
            b = c * CHUNK + q
            return b, isinstance(b, int) and b == BLOCKS - 1

        assert CHUNK == 4
        BESIDE_NORM = 6
        TO_MEAN, TO_OWN, TO_SLOPE = 4, 6, 7
        TO_LAST = 64

        block_ctx = ctx.enter_context(nc.Block())

        @block_ctx.sync
        def _(sp):
            first_credit(sp, ["stored"])
            sp.dma_start(dst_i, dst.rearrange("(p e) -> p e", p=EP)).then_inc(ld_dst, 16)

            def load_group(g):
                if g >= RING:
                    done(sp, a_norm, GROUP * (g - RING + 1))
                if g < GROUPS - 1:
                    sp.dma_start(xgroup[g % RING], x[g * GROUP * P:(g + 1) * GROUP * P, :].rearrange(
                        "(t p) d -> p t d", p=P)).then_inc(ld_xg[g % RING], 16)
                else:
                    r0 = g * GROUP * P
                    sp.dma_start(xgroup[g % RING][:, 0:GROUP - 1], x[r0:r0 + (GROUP - 1) * P, :].rearrange(
                        "(t p) d -> p t d", p=P)).then_inc(ld_xg[g % RING], 16)
                    sp.dma_start(xgroup[g % RING][0:LAST, GROUP - 1], x[N - LAST:N, :]).then_inc(ld_xg[g % RING], 16)

            load_group(0)
            load_group(1)
            sp.dma_start(src_pad[0:E].rearrange("(p e) -> p e", p=EP), src.rearrange("(p e) -> p e", p=EP)).then_inc(ld_pads, 16)
            sp.wait_ge(pool_c, 1)
            sp.dma_start(src_pad[E:E + PASS].rearrange("(p e) -> p e", p=P), padi[:, :]).then_inc(ld_pads, 16)
            sp.dma_start(dst_pad[E:E + PASS].rearrange("(p e) -> p e", p=P), padf[:, :]).then_inc(ld_pads, 16)
            sp.wait_ge(v_dst, 1)
            sp.dma_start(dst_pad[0:E].rearrange("(p e) -> p e", p=EP), dst_f).then_inc(ld_pads, 16)
            sp.dma_start(brow[:, 0, :], b_self.rearrange("(a d) -> a d", a=1)).then_inc(ld_bias, 16)
            sp.wait_ge(v_rng, 1)
            load_group(2)
            load_group(3)
            sp.dma_start(gamma_b[:, :], gamma.rearrange("(a d) -> a d", a=1).broadcast_to((P, D))).then_inc(ld_const, 16)
            sp.dma_start(beta_b[:, :], beta.rearrange("(a d) -> a d", a=1).broadcast_to((P, D))).then_inc(ld_const, 16)
            sp.dma_start(alpha_c[:, :], alpha.rearrange("(a d) -> a d", a=1).broadcast_to((P, 1))).then_inc(ld_const, 16)
            sp.dma_start(wself[:, :, :], W_self.rearrange("(k p) n -> p k n", p=P)).then_inc(ld_const, 16)
            sp.dma_start(wneigh[:, :, :], W_neigh.rearrange("(k p) n -> p k n", p=P)).then_inc(ld_const, 16)
            sp.wait_ge(v_bias, 1)
            for i in range(3):
                sp.dma_start(bparts[i:i + 1, :], browb[:, i, :]).then_inc(ld_bias, 16)
            sp.dma_start(wstage, w_gate.rearrange("(i p) (g k) -> p i g k", p=P, k=P)).then_inc(ld_w[0], 16)
            for g in range(GROUPS):
                if g + RING < GROUPS:
                    load_group(g + RING)
                done(sp, v_low, GROUP * (g + 1))
                if g < GROUPS - 1:
                    sp.dma_start(table[g * GROUP * P:(g + 1) * GROUP * P, :].rearrange("(t p) d -> p t d", p=P),
                                 tstage[g % 2]).then_inc(st_t[g % 2], 16)
                else:
                    r0 = g * GROUP * P
                    sp.dma_start(table[r0:r0 + (GROUP - 1) * P, :].rearrange("(t p) d -> p t d", p=P),
                                 tstage[g % 2][:, 0:GROUP - 1]).then_inc(st_t[g % 2], 16)
                    sp.dma_start(table[N - LAST:N, :], tstage[g % 2][0:LAST, GROUP - 1]).then_inc(st_t[g % 2], 16)
            sp.wait_ge(ld_pads, 64)
            sp.wait_ge(v_rngi, 1)
            passes = sp.alloc_register("sp_passes")
            sp.reg_mov(passes, 0)

            def edges_range(b):
                return (sp.value_load(rangei[0:1, bass.ds(b, 1)], min_val=0, max_val=E),
                        sp.value_load(rangei[0:1, bass.ds(b + BLOCKS, 1)], min_val=0, max_val=E))

            def load_pass(at):
                n = sp.snap(passes)
                sp.wait_ge(p_used, n * LOADS + LOADS)
                sp.sem_inc(sp_turn, 1)
                done(sp, v_dl, n)
                sp.sem_inc(sp_turn, 1)
                sp.dma_start(idx[:, :], src_pad[bass.ds(at, PASS)].rearrange("(p e) -> p e", p=P)).then_inc(ld_idx, 16)
                sp.dma_start(dstv[:, :], dst_pad[bass.ds(at, PASS)].rearrange("(p e) -> p e", p=P)).then_inc(ld_dv, 16)
                sp.reg_add(passes, passes, 1)

            def load_first_pass(b):
                load_pass(edges_range(b)[0])

            def load_more_passes(b):
                first, end = edges_range(b)
                with sp.If(end > first + PASS):
                    with sp.Fori(first + PASS, end, PASS) as at:
                        load_pass(at)

            def load_x(b, q):
                last = isinstance(b, int) and b == BLOCKS - 1
                row = b * P if isinstance(b, int) else sp.snap(b * P)
                done(sp, a_xx, max(b - 1, 0) if isinstance(b, int) else b - 1)
                if last:
                    sp.dma_start(xin[0:LAST, q % 2], x[N - LAST:N, :]).then_inc(ld_x[q % 2], 16)
                else:
                    sp.dma_start(xin[:, q % 2], x[bass.ds(row, P), :]).then_inc(ld_x[q % 2], 16)

            load_x(0, 0)
            load_first_pass(0)
            load_more_passes(0)

            def store_out(c, q, rows_):
                row = (c * CHUNK + q) * P if isinstance(c, int) else sp.snap((c * CHUNK + q) * P)
                done(sp, v_out, c * CHUNK + q + 1)
                sp.dma_start(out[bass.ds(row, rows_), :], outb[0:rows_, q % 2]).then_inc(st_out, 16)
                sp.wait_ge(st_out, c * (16 * CHUNK) + (16 * q + 16))
                sp.sem_inc(stored, 1)

            def block(c, q, par, first, second):
                b, last = number(c, q)
                if not last:
                    load_x(b + 1, q + 1)
                    load_first_pass(b + 1)
                if q == 0 and len(first[2]):
                    for t in range(CHUNK):
                        store_out(first[0], t, P)
                if isinstance(b, int) and b < 2:
                    sp.wait_ge(v_cmp, (b + 1) * FT)
                    rows_of = (w_up.rearrange("(i p) (g k) -> p i g k", p=P, k=P),
                               w_down.rearrange("(i p) (g k) -> p i g k", p=P, k=P))[b]
                    sp.dma_start(wstage, rows_of).then_inc(ld_w[b + 1], 16)
                if not last:
                    load_more_passes(b + 1)

            main(sp, block)
            for t in range(CHUNK):
                store_out(FULL - 1, t, P)
            store_out(FULL, 0, LAST)

        @block_ctx.gpsimd
        def _(pool):
            pool.memset(padi[:, :], 0)
            pool.memset(padf[:, :], -1.0).then_inc(pool_c, 1)
            pool.memset(ones[:, :], 1.0)
            pool.memset(onesb[:, :], 1.0)
            pool.memset(zeros[:, :], 0.0)
            pool.memset(xin[:, :, :], 0.0)
            pool.memset(ranges[:, :], 0.0)
            pool.memset(identf[:, :], 0.0)
            pool.memset(ident[:, :, :], 0.0).then_inc(pool_c, 1)
            pool.iota(rangei[:, 0:BLOCKS], pattern=[[P, BLOCKS]], base=0, channel_multiplier=0)
            pool.iota(posi[:, :], pattern=[[SEG, NSEG]], base=0, channel_multiplier=EROW)
            pool.iota(node_j[:, :, :], pattern=[[1, P], [0, STEPS]], base=0, channel_multiplier=0,
                      allow_small_or_imprecise_dtypes=True)
            pool.wait_ge(pool_c, 2)
            pool.affine_select(out=identf[:, :], in_=identf[:, :], compare_op=ALU.not_equal, fill=1.0, base=0,
                               pattern=[[-1, P]], channel_multiplier=1)
            pool.affine_select(out=ident[:, 0, :], in_=ident[:, 0, :], compare_op=ALU.not_equal, fill=1.0, base=0,
                               pattern=[[-1, P]], channel_multiplier=1)
            pool.affine_select(out=ident[:, 1, :], in_=ident[:, 1, :], compare_op=ALU.not_equal, fill=-1.0, base=0,
                               pattern=[[-1, P]], channel_multiplier=1).then_inc(pool_c, 1)
            pool.wait_ge(v_rng, 1)
            pool.partition_all_reduce(rangem[:, :], ranges[:, :], P, RMAX).then_inc(pool_rng, 1)
            pool.wait_ge(v_rngi, 1)
            pool.wait_ge(st_t[0], 16 * ((GROUPS + 1) // 2) + 16 * (GROUPS % 2))
            pool.wait_ge(st_t[1], 16 * (GROUPS // 2) + 16 * ((GROUPS + 1) % 2))
            passes = pool.alloc_register("pool_passes")
            pool.reg_mov(passes, 0)

            def gather_pass():
                n = pool.snap(passes)
                pool.wait_ge(ld_idx, n * 16 + 16)
                for load in range(LOADS):
                    pool.wait_ge(p_used, n * LOADS + (load + 1))
                    pool.sem_inc(pool_turn, 1)
                    for j in range(load * PER_LOAD, (load + 1) * PER_LOAD):
                        pool.indirect_dma_start(
                            out=rows[:, j, :], out_offset=None, in_=table[:, :],
                            in_offset=bass.IndirectOffsetOnAxis(ap=idx[:, j:j + 1], axis=0)).then_inc(gathered[load], 16)
                pool.reg_add(passes, passes, 1)

            def gather(b):
                gather_pass()
                more_passes(pool, b, gather_pass)

            gather(0)

            def block(c, q, par, first, second):
                b, last = number(c, q)
                if isinstance(b, int) and b == 2:
                    pool.wait_ge(v_max, 1)
                    pool.partition_all_reduce(wmaxa[:, :], wmax[:, :], P, RMAX).then_inc(pool_max, 1)
                if not last:
                    gather(b + 1)

            main(pool, block)

        @block_ctx.tensor
        def _(pe):
            first_credit(pe, ["p_t1", "p_agg", "p_t2", "p_h", "p_t3", "p_up", "p_dn", "p_t4"])
            pe.sem_inc(p_used, LOADS)
            pe.wait_ge(pool_c, 3)

            def turn_weights(w, a, b):
                for n in range(w * FT + a, w * FT + b):
                    pe.wait_ge(v_cmp, n + 1)
                    done(pe, a_tern, max(n + 1 - len(f_ps), 0))
                    for g in range(KT):
                        to = f_ps[n % 4][:, g * P:(g + 1) * P]
                        pe.matmul(to, wcmp[:, n % WRING, 0, g, :], ident[:, 0, :], start=True, stop=False)
                        mm = pe.matmul(to, wcmp[:, n % WRING, 1, g, :], ident[:, 1, :], start=False, stop=True)
                    mm.then_inc(p_tern, 1)

            pe.wait_ge(ld_const, 80)
            pe.wait_ge(ld_bias, 64)
            done(pe, v_low, BLOCKS)
            passes = pe.alloc_register("pe_passes")
            pe.reg_mov(passes, 0)

            def transpose4(source, to=tr_ps):
                for k in range(KT):
                    mm = pe.transpose(to[:, k * P:(k + 1) * P], source(k), identf[:, :])
                return mm

            def step(ffn, s, width=CW):
                c, par = ffn[0], ffn[1]
                kind, i, g, w = place(s)
                to = f_ps[s % 4][:, 0:width]
                if kind == "up":
                    if g >= 2:
                        if g == 2:
                            done(pe, a_up, c * A_UP + (2 * i + w + 1))
                        else:
                            done(pe, v_up, c * V_UP + nth_v_up(i, g - 2, w))
                    elif i:
                        done(pe, v_up, c * V_UP + nth_v_up(i - 1, g + 2, w))
                    else:
                        done(pe, v_dn, c * V_DOWN)
                    lhs, parts = tern[:, w, i * KT + g, :], [x1T[:, par, part, g, 0:width] for part in range(2)]
                    ready = p_up
                else:
                    if g >= 2:
                        if g == 2:
                            done(pe, a_dn, c * A_DOWN + (2 * i + w + 1))
                        else:
                            done(pe, v_dn, c * V_DOWN + nth_v_down(i, g - 2, w))
                    elif i:
                        done(pe, v_dn, c * V_DOWN + nth_v_down(i - 1, FT - 2 + g, w))
                    else:
                        done(pe, v_up, c * V_UP + nth_v_up(FT - 1, g + 2, w))
                    if i == 0:
                        done(pe, v_lo, c * FT + (g + 1))
                    lhs, parts = tern[:, 2, (2 * i + w) * FT + g, :], [hT[:, part, g, 0:width] for part in range(2)]
                    ready = p_dn
                pe.matmul(to, lhs, parts[0], start=True, stop=False)
                pe.matmul(to, lhs, parts[1], start=False, stop=True).then_inc(ready, 1)

            def steps(ffn, a, b, width=CW):
                for s in ffn[2][a:b]:
                    step(ffn, s, width)

            def turn_out(c, t):
                done(pe, v_dn, c * V_DOWN + V_DOWN)
                done(pe, v_out, c * CHUNK + t)
                transpose4(lambda k: yT[:, k, t * P:(t + 1) * P], agg_ps).then_inc(p_t4, 1)

            def turn_x1(b):
                done(pe, a_x1s, b + 1)
                transpose4(lambda k: x1s[:, k * P:(k + 1) * P]).then_inc(p_t3, 1)

            def turned_x1(b):
                done(pe, v_lo1, b + 1)
                done(pe, a_hi1, b + 1)

            def turn_own(b):
                done(pe, a_xs, b + 1)
                transpose4(lambda k: xs[:, k * P:(k + 1) * P]).then_inc(p_t1, 1)

            def sum_load(n, load):
                pe.wait_ge(gathered[load], n * (16 * PER_LOAD) + 16 * PER_LOAD)
                for j in range(load * PER_LOAD, (load + 1) * PER_LOAD):
                    pe.matmul(tr_ps[:, 0:1], hot[:, :, j], ones[:, 0:1], start=False, stop=False, skip_group_check=True)
                    for part in range(2):
                        mm = pe.matmul(agg_ps[:, :], hot[:, :, j], rows[:, j, part * D:(part + 1) * D],
                                       start=False, stop=False, skip_group_check=True)
                mm.then_inc(p_used, 1)

            def sum_pass():
                n = pe.snap(passes)
                done(pe, v_hot, n + 1)
                for load in range(LOADS):
                    sum_load(n, load)
                pe.reg_add(passes, passes, 1)

            def block(c, q, par, first, second):
                b, last = number(c, q)
                done(pe, a_ng, b)
                done(pe, a_xsT, b + 1)
                pe.matmul(agg_ps[:, 0:1], zeros[:, :], zeros[:, 0:1], start=True, stop=False, skip_group_check=True)
                pe.matmul(tr_ps[:, 0:1], zeros[:, :], zeros[:, 0:1], start=True, stop=False, skip_group_check=True)
                n = pe.snap(passes)
                done(pe, v_hot, n + 1)
                for load in range(LOADS):
                    sum_load(n, load)
                    steps(first, IN_SUM * load // LOADS, IN_SUM * (load + 1) // LOADS)
                    if isinstance(b, int) and b < 3:
                        turn_weights(b, FT * load // LOADS, FT * (load + 1) // LOADS)
                pe.reg_add(passes, passes, 1)
                more_passes(pe, b, sum_pass)
                pe.matmul(agg_ps[:, 0:1], zeros[:, :], zeros[:, 0:1], start=False, stop=True, skip_group_check=True)
                pe.matmul(tr_ps[:, 0:1], zeros[:, :], zeros[:, 0:1], start=False, stop=True,
                          skip_group_check=True).then_inc(p_agg, 1)
                done(pe, v_x1, b)
                pe.matmul(h_ps[:, :], onesb[:, :], bparts[:, :], start=True, stop=False)
                behind = not (isinstance(b, int) and b == 0)
                for k in range(KT):
                    if k == KT - 1:
                        done(pe, v_inv, b + 1)
                        if behind:
                            turn_x1(b - 1)
                    pe.matmul(h_ps[:, :], xsT[:, k, :], wself[:, k, :], start=False, stop=False)
                    steps(first, BY_OWN[k], BY_OWN[k + 1])
                if q == 0 and behind:
                    turned_x1(b - 1)
                steps(second, 0, TO_MEAN)
                if q and behind:
                    turned_x1(b - 1)
                done(pe, a_ng, b + 1)
                transpose4(lambda k: ng[:, k * P:(k + 1) * P]).then_inc(p_t2, 1)
                steps(second, TO_MEAN, TO_OWN)
                done(pe, a_ngT, b + 1)
                for k in range(KT):
                    if q == 0 and len(first[2]):
                        turn_out(first[0], k)
                    mm = pe.matmul(h_ps[:, :], ngT[:, k, :], wneigh[:, k, :], start=False, stop=(k == KT - 1))
                    if k == KT - 1:
                        mm.then_inc(p_h, 1)
                    rest = len(second[2]) - TO_OWN
                    steps(second, TO_OWN + rest * k // KT, TO_OWN + rest * (k + 1) // KT)
                    if k == 1 and not last:
                        turn_own(b + 1)
                if q == 0 and len(first[2]):
                    done(pe, v_out, first[0] * CHUNK + CHUNK)

            turn_own(0)
            main(pe, block)
            rest = (FULL - 1, 1, range(QUARTER - LATE, ALL))
            steps(rest, 0, TO_LAST)
            done(pe, a_ngT, BLOCKS)
            turn_x1(BLOCKS - 1)
            turned_x1(BLOCKS - 1)
            steps(rest, TO_LAST, ALL)
            for t in range(CHUNK):
                turn_out(FULL - 1, t)
            steps((FULL, 0, range(ALL)), 0, ALL, P)
            turn_out(FULL, 0)

        @block_ctx.scalar
        def _(act):
            first_credit(act, ["a_norm", "a_high", "a_tern", "a_xs", "a_xx", "a_xsT", "a_ng", "a_ngT", "a_y", "a_x1s",
                               "a_hi1", "a_up", "a_silu", "a_hi", "a_dn"])
            def normalised(i):
                g, t = divmod(i, GROUP)
                if t == 0:
                    act.wait_ge(v_stat, g + 1)
                done(act, v_low, max(i + 1 - len(nbank), 0))
                act.activation(nbank[i % len(nbank)][:, :], xgroup[g % RING][:, t, :], ACT.Identity, bias=nmr_k[:, i:i + 1],
                               scale=rstd_k[:, i:i + 1]).then_inc(a_norm, 1)

            normalised(0)
            for i in range(BLOCKS):
                g, t = divmod(i, GROUP)
                if i + 1 < BLOCKS:
                    normalised(i + 1)
                if g >= 2 and t == 0:
                    act.wait_ge(st_t[g % 2], 16 * (g // 2))
                done(act, a_norm, i + 1)
                act.activation(tstage[g % 2][:, t, 0:D], nbank[i % len(nbank)][:, :], ACT.Copy).then_inc(a_high, 1)

            def keep_weights(w):
                for i in range(FT):
                    n = w * FT + i
                    act.wait_ge(p_tern, n + 1)
                    act.activation(tern[:, w, i * KT:(i + 1) * KT, :].rearrange("p g k -> p (g k)"), f_ps[n % 4][:, :],
                                   ACT.Copy).then_inc(a_tern, 1)

            act.wait_ge(ld_const, 80)

            def step(ffn, s, width=CW):
                c = ffn[0]
                kind, i, g, w = place(s)
                if kind == "up" and g == 0:
                    act.wait_ge(p_up, c * UP_STEPS + (s + 2))
                    act.activation(acc[:, w, i % 2, 0:width], f_ps[s % 4][:, 0:width], ACT.Copy,
                                   scale=scl[:, w, i * KT:i * KT + 1]).then_inc(a_up, 1)
                if kind == "up" and g == KT - 1 and w == 1:
                    done(act, v_up, c * V_UP + nth_v_up(i, KT - 1, 0))
                    done(act, v_lo, c * FT + i)
                    act.activation(misc_ps[:, 0:width], acc[:, 0, i % 2, 0:width], ACT.Silu).then_inc(a_silu, 1)
                if kind == "down" and g == 0:
                    act.wait_ge(p_dn, c * DOWN_STEPS + (s - UP_STEPS + 2))
                    if i == 0:
                        done(act, p_t4, c * CHUNK)
                    d = 2 * i + w
                    act.activation(yT[:, d, 0:width], f_ps[s % 4][:, 0:width], ACT.Copy,
                                   scale=scl[:, 2, d * FT:d * FT + 1]).then_inc(a_dn, 1)
                if s % (2 * KT) == 5 and 0 < s <= UP_STEPS + 5:
                    f = s // (2 * KT) - 1
                    if f >= 0:
                        done(act, v_h, c * FT + (f + 1))
                        act.activation(hT[:, 0, f, 0:width], misc_ps[:, 0:width], ACT.Copy).then_inc(a_hi, 1)

            def steps(ffn, a, b, width=CW):
                for s in ffn[2][a:b]:
                    step(ffn, s, width)

            def slope(b):
                done(act, v_t2, b + 1)
                act.activation(neg[:, :], t2[:, :], ACT.Relu, scale=-1.0)
                act.activation(h_ps[:, :], t2[:, :], ACT.Relu).then_inc(a_y, 1)

            def norm_x1(b, q, par):
                done(act, v_n1, b + 1)
                done(act, p_t3, b)
                act.activation(x1s[:, :], x1[:, par, q, :], ACT.Identity, bias=small[:, 13:14],
                               scale=small[:, 10:11]).then_inc(a_x1s, 1)

            def high_x1(b, q, par):
                done(act, p_t3, b + 1)
                act.activation(x1T[:, par, 0, :, q * P:(q + 1) * P], tr_ps[:, :].rearrange("p (k n) -> p k n", k=KT),
                               ACT.Copy, scale=XSCALE).then_inc(a_hi1, 1)

            def own_rows(b, q):
                act.wait_ge(ld_x[q % 2], (b // 2 + 1) * 16 if isinstance(b, int) else (b - q % 2) * 8 + 16)
                done(act, p_t1, b)
                act.activation(xs[:, :], xin[:, q % 2, :], ACT.Identity, bias=nmr[:, bass.ds(b, 1)],
                               scale=rstd[:, bass.ds(b, 1)]).then_inc(a_xs, 1)
                done(act, v_x1, max(b - 1, 0) if isinstance(b, int) else b - 1)
                act.activation(xx[:, q % 2, :], xin[:, q % 2, :], ACT.Identity, bias=nmr[:, bass.ds(b, 1)],
                               scale=one_r[:, bass.ds(b, 1)]).then_inc(a_xx, 1)

            def own_turned(b):
                done(act, p_t1, b + 1)
                done(act, p_t2, b)
                act.activation(xsT[:, :, :].rearrange("p k n -> p (k n)"), tr_ps[:, :], ACT.Copy).then_inc(a_xsT, 1)

            def block(c, q, par, first, second):
                b, last = number(c, q)
                behind = not (isinstance(b, int) and b == 0)
                at = ((q - 1) % CHUNK, par if q else 1 - par)
                if isinstance(b, int) and b < 3:
                    keep_weights(b)
                if isinstance(b, int) and b == CHUNK:
                    act.wait_ge(v_scl, 1)
                steps(first, 0, TO_SLOPE)
                if behind:
                    slope(b - 1)
                steps(first, TO_SLOPE, IN_SUM)
                if behind:
                    norm_x1(b - 1, *at)
                done(act, p_agg, b + 1)
                done(act, v_inv, b + 1)
                done(act, p_t2, b)
                act.activation(ng[:, :], agg_ps[:, :], ACT.Copy, scale=small[:, 1:2]).then_inc(a_ng, 1)
                steps(first, IN_SUM, LATE)
                if behind:
                    high_x1(b - 1, *at)
                steps(second, 0, TO_MEAN)
                done(act, p_t2, b + 1)
                act.activation(ngT[:, :, :].rearrange("p k n -> p (k n)"), tr_ps[:, :], ACT.Copy).then_inc(a_ngT, 1)
                steps(second, TO_MEAN, TO_OWN)
                if not last:
                    own_rows(b + 1, q + 1)
                half = TO_OWN + (QUARTER - LATE - TO_OWN) // 2
                steps(second, TO_OWN, half)
                if not last:
                    own_turned(b + 1)
                steps(second, half, QUARTER)

            own_rows(0, 0)
            own_turned(0)
            main(act, block)
            rest = (FULL - 1, 1, range(QUARTER - LATE, ALL))
            steps(rest, 0, TO_SLOPE)
            slope(BLOCKS - 1)
            steps(rest, TO_SLOPE, LATE)
            norm_x1(BLOCKS - 1, 0, 0)
            steps(rest, LATE, TO_LAST)
            high_x1(BLOCKS - 1, 0, 0)
            steps(rest, TO_LAST, ALL)
            steps((FULL, 0, range(ALL)), 0, ALL, P)

        @block_ctx.vector
        def _(dve):
            first_credit(dve, ["v_low", "v_dl", "v_hot", "v_deg", "v_inv", "v_t2", "v_x1", "v_n1", "v_lo1", "v_up", "v_h",
                               "v_lo", "v_dn", "v_out"])

            class Chain:

                def __init__(self, s, start=0):
                    self.s, self.n, self.start = s, 0, start

                def step(self, ins, fill=None):
                    ins.then_inc(self.s, 1)
                    self.n += 1
                    if fill is not None:
                        fill()
                    dve.wait_ge(self.s, self.start + self.n)

            def rsqrt(chain, v, y, a, vh, yc, fill=None):
                chain.step(dve.tensor_scalar(a, v, EPS, None, ALU.add))
                dve.tensor_scalar(vh, a, 64.0 / 9.0, None, ALU.mult)
                chain.step(dve.tensor_scalar(y.bitcast(I32), a.bitcast(I32), -0.5, RSQRT_GUESS, ALU.mult, ALU.add))
                if y.shape[-1] == 1:
                    dve.tensor_scalar(yc, y, RSQRT_GAIN * 3.0 / 8.0, None, ALU.mult)
                    chain.step(dve.tensor_scalar(a, y, y, a, ALU.mult, ALU.mult), fill)
                else:
                    dve.tensor_scalar(yc, y, RSQRT_GAIN * 3.0 / 8.0, None, ALU.mult)
                    chain.step(dve.tensor_tensor(y, y, y, ALU.mult))
                    chain.step(dve.tensor_tensor(a, a, y, ALU.mult))
                chain.step(dve.scalar_tensor_tensor(out=yc, in0=a, scalar=RSQRT_FIRST, in1=yc, op0=ALU.subtract,
                                                    op1=ALU.mult), fill)
                if y.shape[-1] == 1:
                    chain.step(dve.tensor_scalar(a, yc, yc, vh, ALU.mult, ALU.mult))
                else:
                    chain.step(dve.tensor_tensor(a, yc, yc, ALU.mult))
                    chain.step(dve.tensor_tensor(a, a, vh, ALU.mult))
                chain.step(dve.scalar_tensor_tensor(out=a, in0=a, scalar=10.0 / 3.0, in1=a, op0=ALU.subtract, op1=ALU.mult))
                chain.step(dve.scalar_tensor_tensor(out=y, in0=a, scalar=5.0, in1=yc, op0=ALU.add, op1=ALU.mult), fill)

            pro = Chain(v_pro)
            dve.wait_ge(ld_dst, 16)
            pro.step(dve.tensor_copy(dst_f, dst_i))
            dve.sem_inc(v_dst, 1)
            seg3 = dst_f.rearrange("p (s e) -> p s e", e=SEG)
            dve.tensor_reduce(segs[0:EP, 0, :], seg3, AX.X, ALU.min)
            dve.tensor_reduce(segs[0:EP, 1, :], seg3, AX.X, ALU.max)
            dve.wait_ge(pool_c, 3)
            dve.tensor_copy(base[:, :], rangei[:, 0:BLOCKS])
            pro.step(dve.tensor_scalar(top[:, :], rangei[:, 0:BLOCKS], float(P - 1), None, ALU.add))
            dve.tensor_scalar(segs[:, 2, :], posi[:, :], -1.0, BIG, ALU.mult, ALU.add)
            pro.step(dve.tensor_scalar(segs[:, 3, :], posi[:, :], float(SEG), None, ALU.add))

            def over_blocks(v):
                return v[0:EP, None, :].broadcast_to((EP, BLOCKS, NSEG))

            def over_segs(v):
                return v[0:EP, :, None].broadcast_to((EP, BLOCKS, NSEG))

            dve.tensor_tensor(hit[0], over_blocks(segs[:, 0, :]), over_segs(top[:, :]), ALU.is_le)
            pro.step(dve.tensor_tensor(hit[1], over_blocks(segs[:, 1, :]), over_segs(base[:, :]), ALU.is_ge))
            pro.step(dve.tensor_tensor(hit[0], hit[0], hit[1], ALU.mult))
            dve.tensor_tensor(hit[1], hit[0], over_blocks(segs[:, 2, :]), ALU.mult)
            pro.step(dve.tensor_tensor(hit[2], hit[0], over_blocks(segs[:, 3, :]), ALU.mult))
            dve.tensor_reduce(ranges[0:EP, 0:BLOCKS], hit[1], AX.X, ALU.max)
            dve.tensor_reduce(ranges[0:EP, BLOCKS:2 * BLOCKS], hit[2], AX.X, ALU.max).then_inc(v_rng, 1)
            dve.wait_ge(ld_bias, 16)
            for i in range(3):
                pro.step(dve.tensor_copy(browb[:, i, :], brow[:, i, :]))
                if i < 2:
                    pro.step(dve.tensor_tensor(brow[:, i + 1, :], brow[:, i, :], browb[:, i, :], ALU.subtract))
            dve.sem_inc(v_bias, 1)
            dve.wait_ge(pool_rng, 1)
            pro.step(dve.tensor_scalar(rangem[:, 0:BLOCKS], rangem[:, 0:BLOCKS], -1.0, BIG, ALU.mult, ALU.add))
            pro.step(dve.tensor_scalar(rangem[:, 0:BLOCKS], rangem[:, 0:BLOCKS], float(E), None, ALU.min))
            pro.step(dve.scalar_tensor_tensor(out=ranges[:, 0:BLOCKS], in0=rangem[:, BLOCKS:2 * BLOCKS], scalar=-float(PASS),
                                              in1=rangem[:, 0:BLOCKS], op0=ALU.add, op1=ALU.subtract))
            pro.step(dve.tensor_scalar(ranges[:, 0:BLOCKS], ranges[:, 0:BLOCKS], 0.0, None, ALU.max))
            dve.tensor_copy(rangei[:, 0:2 * BLOCKS], rangem[:, :])
            dve.tensor_copy(rangei[:, 2 * BLOCKS:3 * BLOCKS], ranges[:, 0:BLOCKS]).then_inc(v_rngi, 1)

            loaded = [0] * RING

            def group_stats(g):
                loaded[g % RING] += 32 if g == GROUPS - 1 else 16
                dve.wait_ge(ld_xg[g % RING], loaded[g % RING])
                lo, hi = g * GROUP, (g + 1) * GROUP
                for t in range(GROUP):
                    ins = dve.bn_stats(stats6[:, t, :], xgroup[g % RING][:, t, :])
                pro.step(ins)
                for t in range(GROUP):
                    ins = dve.bn_aggr(mv[:, lo + t, :], stats6[:, t, :])
                pro.step(ins)
                rsqrt(pro, mv[:, lo:hi, 1], rstd[:, lo:hi], tmp[:, 0, :], tmp[:, 1, :], tmp[:, 2, :])
                dve.tensor_scalar(rstd_k[:, lo:hi], rstd[:, lo:hi], XSCALE, None, ALU.mult)
                dve.tensor_scalar(one_r[:, lo:hi], rstd[:, lo:hi], 1.0, None, ALU.add)
                pro.step(dve.scalar_tensor_tensor(out=nmr[:, lo:hi], in0=mv[:, lo:hi, 0], scalar=-1.0,
                                                  in1=rstd[:, lo:hi], op0=ALU.mult, op1=ALU.mult))
                dve.tensor_scalar(nmr_k[:, lo:hi], nmr[:, lo:hi], XSCALE, None, ALU.mult).then_inc(v_stat, 1)

            def group_low(g):
                for t in range(GROUP):
                    i = g * GROUP + t
                    done(dve, a_high, i + 1)
                    dve.tensor_tensor(tstage[g % 2][:, t, D:2 * D], nbank[i % len(nbank)][:, :], tstage[g % 2][:, t, 0:D],
                                      ALU.subtract).then_inc(v_low, 1)

            group_stats(0)
            for g in range(GROUPS):
                if g + 1 < GROUPS:
                    group_stats(g + 1)
                group_low(g)

            passes = dve.alloc_register("dve_passes")
            dve.reg_mov(passes, 0)

            def one_hot_pass(b):
                n = dve.snap(passes)
                dve.wait_ge(ld_dv, n * 16 + 16)
                done(dve, v_hot, n)
                dve.tensor_scalar(dstl[:, :], dstv[:, :], base[:, bass.ds(b, 1)], None, ALU.subtract).then_inc(v_dl, 1)
                done(dve, v_dl, n + 1)
                dve.wait_ge(p_used, n * LOADS + LOADS)
                dve.tensor_tensor(hot[:, :, :], dstl[:, None, :].broadcast_to((P, P, STEPS)), node_j[:, :, :],
                                  ALU.is_equal).then_inc(v_hot, 1)
                dve.reg_add(passes, passes, 1)

            one_hot_pass(0)

            def weight_scales(w):
                dve.wait_ge(ld_w[w], 16)
                pro.step(dve.tensor_reduce(scl[:, w, :], wstage, AX.X, ALU.add, apply_absolute_value=True))
                pro.step(dve.tensor_scalar(scl[:, w, :], scl[:, w, :], 1.0 / P, EPS, ALU.mult, ALU.add))
                dve.tensor_scalar(half[:, 0, :], scl[:, w, :], 0.5, None, ALU.mult)
                pro.step(dve.tensor_scalar(half[:, 1, :], scl[:, w, :], -0.5, None, ALU.mult))
                if w == 0:
                    dve.wait_ge(st_t[0], 16 * ((GROUPS + 1) // 2) + 16 * (GROUPS % 2))
                    dve.wait_ge(st_t[1], 16 * (GROUPS // 2) + 16 * ((GROUPS + 1) % 2))

            def weight_tiles(w, i):
                n = w * FT + i
                if n >= WRING:
                    dve.wait_ge(p_tern, n + 1 - WRING)
                for g in range(KT):
                    j = i * KT + g
                    dve.tensor_scalar(wcmp[:, n % WRING, 0, g, :], wstage[:, j, :], half[:, 0, j:j + 1], None, ALU.is_gt)
                    ins = dve.tensor_scalar(wcmp[:, n % WRING, 1, g, :], wstage[:, j, :], half[:, 1, j:j + 1], None, ALU.is_lt)
                ins.then_inc(v_cmp, 1)

            def largest_scales():
                dve.tensor_reduce(wmax[:, 0:1], scl[:, 0, :], AX.X, ALU.max)
                dve.tensor_reduce(wmax[:, 1:2], scl[:, 1, :], AX.X, ALU.max).then_inc(v_max, 1)

            def hidden_scale():
                dve.wait_ge(pool_max, 1)
                pro.step(dve.tensor_scalar(hsc[:, 0:1], wmaxa[:, 0:1], wmaxa[:, 1:2], float(D * D) / 2.0 ** 15, ALU.mult, ALU.mult))
                pro.step(dve.reciprocal(hsc[:, 1:2], hsc[:, 0:1]))
                pro.step(dve.tensor_scalar(hsc[:, 2:3].bitcast(I32), hsc[:, 1:2].bitcast(I32), EXPONENT_BITS, None, ALU.bitwise_and))
                pro.step(dve.tensor_scalar(hsc[:, 3:4].bitcast(I32), hsc[:, 2:3].bitcast(I32), -1.0, TWICE_BIAS_BITS, ALU.mult, ALU.add))
                dve.tensor_scalar(scl[:, 0, :], scl[:, 0, :], 1.0 / XSCALE, None, ALU.mult)
                dve.tensor_scalar(scl[:, 1, :], scl[:, 1, :], hsc[:, 2:3], 1.0 / XSCALE, ALU.mult, ALU.mult)
                pro.step(dve.tensor_scalar(scl[:, 2, :], scl[:, 2, :], hsc[:, 3:4], None, ALU.mult))
                dve.sem_inc(v_scl, 1)

            dve.wait_ge(ld_const, 80)
            pro.step(dve.tensor_scalar(neg_alpha[:, :], alpha_c[:, :], -1.0, None, ALU.mult))

            def step(ffn, s, width=CW):
                c = ffn[0]
                kind, i, g, w = place(s)
                ps = f_ps[s % 4][:, 0:width]
                if kind == "up" and g:
                    dve.wait_ge(p_up, c * UP_STEPS + (s + 2))
                    if g == 1:
                        done(dve, a_up, c * A_UP + (2 * i + w + 1))
                    else:
                        done(dve, v_up, c * V_UP + nth_v_up(i, g - 1, w))
                    a = acc[:, w, i % 2, 0:width]
                    dve.scalar_tensor_tensor(out=a, in0=ps, scalar=scl[:, w, i * KT + g:i * KT + g + 1], in1=a,
                                             op0=ALU.mult, op1=ALU.add).then_inc(v_up, 1)
                if kind == "down" and g:
                    d = 2 * i + w
                    dve.wait_ge(p_dn, c * DOWN_STEPS + (s - UP_STEPS + 2))
                    if g == 1:
                        done(dve, a_dn, c * A_DOWN + (d + 1))
                    else:
                        done(dve, v_dn, c * V_DOWN + nth_v_down(i, g - 1, w))
                    y = yT[:, d, 0:width]
                    dve.scalar_tensor_tensor(out=y, in0=ps, scalar=scl[:, 2, d * FT + g:d * FT + g + 1], in1=y,
                                             op0=ALU.mult, op1=ALU.add).then_inc(v_dn, 1)
                f = s // (2 * KT) - 1
                if 0 <= f < FT and s % (2 * KT) == 2:
                    done(dve, a_silu, c * FT + (f + 1))
                    done(dve, v_up, c * V_UP + nth_v_up(f, KT - 1, 1))
                    dve.tensor_tensor(misc_ps[:, 0:width], misc_ps[:, 0:width], acc[:, 1, f % 2, 0:width],
                                      ALU.mult).then_inc(v_h, 1)
                if 0 <= f < FT and s % (2 * KT) == 6:
                    done(dve, a_hi, c * FT + (f + 1))
                    dve.tensor_tensor(hT[:, 1, f, 0:width], misc_ps[:, 0:width], hT[:, 0, f, 0:width],
                                      ALU.subtract).then_inc(v_lo, 1)

            def steps(ffn, a, b, width=CW):
                for s in ffn[2][a:b]:
                    step(ffn, s, width)

            def norms(b, q, par, ffn, others=()):
                others = iter(others)
                chain = Chain(v_chain, b * CHAIN_STEPS)
                todo = iter(ffn[2][0:IN_SUM])
                used = [0]

                def fill():
                    for s in todo:
                        step(ffn, s)
                        used[0] += 1
                        return
                    for other in others:
                        weight_tiles(*other)
                        return

                done(dve, p_h, b + 1)
                chain.step(dve.bn_stats(st6[:, :], h_ps[:, :]), fill)
                dve.sem_inc(dve_turn, 1)
                chain.step(dve.bn_aggr(small[:, 2:4], st6[:, :]), fill)
                rsqrt(chain, small[:, 3:4], small[:, 4:5], small[:, 5:6], small[:, 6:7], small[:, 7:8], fill)
                chain.step(dve.scalar_tensor_tensor(out=h_ps[:, :], in0=h_ps[:, :], scalar=small[:, 2:3],
                                                    in1=gamma_b[:, :], op0=ALU.subtract, op1=ALU.mult), fill)
                assert used[0] in (0, TO_SLOPE - 1)
                done(dve, a_y, b)
                dve.scalar_tensor_tensor(out=t2[:, :], in0=h_ps[:, :], scalar=small[:, 4:5], in1=beta_b[:, :],
                                         op0=ALU.mult, op1=ALU.add).then_inc(v_t2, 1)
                fill()
                done(dve, a_y, b + 1)
                done(dve, a_xx, b + 1)
                chain.step(dve.scalar_tensor_tensor(out=xx[:, q % 2, :], in0=neg[:, :], scalar=neg_alpha[:, 0:1],
                                                    in1=xx[:, q % 2, :], op0=ALU.mult, op1=ALU.add), fill)
                dve.tensor_tensor(x1[:, par, q, :], h_ps[:, :], xx[:, q % 2, :], ALU.add).then_inc(v_x1, 1)
                done(dve, v_x1, b + 1)
                chain.step(dve.bn_stats(st6[:, :], x1[:, par, q, :]), fill)
                done(dve, a_x1s, b)
                dve.sem_inc(dve_turn, 1)
                chain.step(dve.bn_aggr(small[:, 8:10], st6[:, :]), fill)
                rsqrt(chain, small[:, 9:10], small[:, 10:11], small[:, 11:12], small[:, 12:13], small[:, 14:15], fill)
                dve.tensor_scalar(small[:, 13:14], small[:, 8:9], small[:, 10:11], -1.0, ALU.mult,
                                  ALU.mult).then_inc(v_n1, 1)
                assert chain.n == CHAIN_STEPS, chain.n
                for s in todo:
                    step(ffn, s)

            def low_x1(b, q, par):
                done(dve, p_t3, b + 1)
                done(dve, a_hi1, b + 1)
                dve.scalar_tensor_tensor(out=x1T[:, par, 1, :, q * P:(q + 1) * P],
                                         in0=tr_ps[:, :].rearrange("p (k n) -> p k n", k=KT), scalar=XSCALE,
                                         in1=x1T[:, par, 0, :, q * P:(q + 1) * P], op0=ALU.mult,
                                         op1=ALU.subtract).then_inc(v_lo1, 1)

            def add_out(c, par, t):
                done(dve, p_t4, c * CHUNK + (t + 1))
                done(dve, stored, c * CHUNK + max(t - 1, 0))
                dve.tensor_tensor(outb[:, t % 2, :], agg_ps[:, :], x1[:, par, t, :], ALU.add).then_inc(v_out, 1)

            def block(c, q, par, first, second):
                b, last = number(c, q)
                behind = not (isinstance(b, int) and b == 0)
                at = ((q - 1) % CHUNK, par if q else 1 - par)
                tiles = []
                if isinstance(b, int) and b < 3:
                    weight_scales(b)
                    tiles = [(b, i) for i in range(FT)]
                    for i in range(FT if b == 0 else FT - BESIDE_NORM):
                        weight_tiles(*tiles.pop(0))
                    if b == 1:
                        largest_scales()
                if isinstance(b, int) and b == 3:
                    hidden_scale()
                if behind:
                    norms(b - 1, *at, first, tiles)
                more_passes(dve, b, lambda: one_hot_pass(b))
                done(dve, p_agg, b + 1)
                done(dve, a_ng, b)
                dve.tensor_scalar(small[:, 0:1], tr_ps[:, 0:1], 1.0, XSCALE, ALU.max, ALU.mult).then_inc(v_deg, 1)
                done(dve, v_deg, b + 1)
                dve.reciprocal(small[:, 1:2], small[:, 0:1]).then_inc(v_inv, 1)
                steps(first, IN_SUM, LATE)
                if behind:
                    low_x1(b - 1, *at)
                steps(second, 0, TO_MEAN)
                steps(second, TO_MEAN, TO_OWN)
                rest = len(second[2]) - TO_OWN
                for k in range(KT):
                    if q == 0 and len(first[2]):
                        add_out(first[0], first[1], k)
                    if rest > 0:
                        steps(second, TO_OWN + rest * k // KT, TO_OWN + rest * (k + 1) // KT)
                    if k == 0 and not last:
                        one_hot_pass(b + 1)

            main(dve, block)
            rest = (FULL - 1, 1, range(QUARTER - LATE, ALL))
            norms(BLOCKS - 1, 0, 0, rest)
            steps(rest, IN_SUM, TO_LAST)
            low_x1(BLOCKS - 1, 0, 0)
            steps(rest, TO_LAST, ALL)
            for t in range(CHUNK):
                add_out(FULL - 1, 1, t)
            steps((FULL, 0, range(ALL)), 0, ALL, P)
            add_out(FULL, 0, 0)


CHAIN_STEPS = 2 * (2 + 7) + 2

_INS = ["x", "src", "dst", "L0_gnn_W_self", "L0_gnn_b_self", "L0_gnn_W_neigh", "L0_gnn_gamma", "L0_gnn_beta",
        "L0_gnn_alpha", "L0_ffn_w_gate", "L0_ffn_w_up", "L0_ffn_w_down"]


def kernel(**inputs):
    import concourse.bacc as bacc
    from concourse.bass_utils import run_bass_kernel_spmd

    nc = bacc.Bacc("TRN2", target_bir_lowering=False, num_devices=1)
    arrays, args = {}, []
    for name in _INS:
        a = np.ascontiguousarray(inputs[name])
        if a.ndim == 0:
            a = a.reshape(1)
        arrays[f"in_{name}"] = a
        args.append(nc.dram_tensor(f"in_{name}", a.shape, mybir.dt.from_np(a.dtype), kind="ExternalInput").ap())
    shape = np.shape(inputs["x"])
    args.append(nc.dram_tensor("out_nodes", shape, F32, kind="ExternalOutput").ap())
    build(nc, *args)
    r = run_bass_kernel_spmd(nc, [arrays], core_ids=[0])
    return r.results[0]["out_nodes"]
```
